# Optimizing a Trainium2 kernel written in Bass

```python
import numpy as np
import jax
import jax.numpy as jnp

def _softmax(x, axis=-1):
    return jax.nn.softmax(x, axis=axis)

def _gelu(x):
    return jax.nn.gelu(x, approximate=True)

def _silu(x):
    return jax.nn.silu(x)

def _sigmoid(x):
    return jax.nn.sigmoid(x)

def _layernorm(x, axis=-1, eps=1e-05):
    m = jnp.mean(x, axis=axis, keepdims=True)
    v = jnp.var(x, axis=axis, keepdims=True)
    return (x - m) / jnp.sqrt(v + eps)

def _scatter_add(tgt, idx, src, axis=0):
    return tgt.at[idx].add(src)

def _segment_sum(src, seg, n):
    return jax.ops.segment_sum(src, seg, n)
kernel_name = 'mk_decoder_postln_d1_seqx_r2_2272ea'

def setup_inputs(seed: int=0):
    np.random.seed(seed)
    _w = jnp.asarray

    def _rec_inputs():
        import jax
        import jax.numpy as jnp
        _rk = jax.random.key(seed)
        x = 7.22e-05 + 1 * jax.random.normal(jax.random.fold_in(_rk, 1), (8, 224, 512), jnp.float32)
        _lenS = 224 - jax.random.randint(jax.random.fold_in(_rk, 7), (8,), 0, max(1, 224 // 4) + 1, jnp.int32)
        _lenS2 = 750 - jax.random.randint(jax.random.fold_in(_rk, 8), (8,), 0, max(1, 750 // 4) + 1, jnp.int32)
        _ctx_1024P = jax.random.normal(jax.random.fold_in(_rk, 11), (8, 16, 512), jnp.float32)
        _ctx_1024c = jax.random.dirichlet(jax.random.fold_in(_rk, 511), 0.3 * jnp.ones((16,), jnp.float32), (8, 750))
        _ctx_1024t = jnp.einsum('bsk,bkd->bsd', _ctx_1024c, _ctx_1024P)
        _ctx_1024t = _ctx_1024t * jax.lax.rsqrt(jnp.mean(jnp.square(_ctx_1024t)) + 1e-12) * 0.953939
        ctx_1024 = 4.13588e-05 + 0.999923 * (_ctx_1024t + 0.3 * jax.random.normal(jax.random.fold_in(_rk, 611), (8, 750, 512), jnp.float32))
        _validS = jnp.arange(224)[None, :] < _lenS[:, None]
        _validS2 = jnp.arange(750)[None, :] < _lenS2[:, None]
        _causal = jnp.tril(jnp.ones((224, 224), dtype=bool))
        mask_BxSxS2_ik1 = jnp.where(jnp.broadcast_to(_validS2[:, None, :], (8, 224, 750)), 1, 0).astype(jnp.int32)
        return (x, ctx_1024, mask_BxSxS2_ik1)
    x, ctx_1024, mask_BxSxS2_ik1 = _rec_inputs()

    def _L0_attn_setup():
        import jax, jax.numpy as jnp
        import numpy as np
        B, N, C, H, W = (2, 1024, 512, 16, 8)
        HD = C // H
        SCALE = HD ** (-0.5)

        def band_mask(n, w):
            i = jnp.arange(n)[:, None]
            j = jnp.arange(n)[None, :]
            lo = jnp.where(i <= w, 0, i - w)
            hi = jnp.where(n - i <= w, n - 1, i + w)
            return (j >= lo) & (j <= hi)
        key = jax.random.key(seed)
        k1, k2, k3 = jax.random.split(key, 3)
        x = jax.random.normal(k1, (B, N, C), dtype=jnp.float32)
        Wqkv = jax.random.normal(k2, (C, 3 * C), dtype=jnp.float32) * C ** (-0.5)
        Wproj = jax.random.normal(k3, (C, C), dtype=jnp.float32) * C ** (-0.5)
        bproj = jnp.zeros((C,), dtype=jnp.float32)
        return {'x': x, 'Wqkv': Wqkv, 'Wproj': Wproj, 'bproj': bproj}
    _L0_attn_all = _L0_attn_setup()
    _L0_attn_in = {k: v for k, v in _L0_attn_all.items() if k in ('Wqkv', 'Wproj', 'bproj')}
    del _L0_attn_all

    def _L0_xattn_setup():
        import jax, jax.numpy as jnp
        import numpy as np
        HID = 512
        HEADS = 16
        HEAD_DIM = HID // HEADS

        def _split_heads(x, W, b):
            B, S, _ = x.shape
            y = x @ W + b
            return y.reshape(B, S, HEADS, HEAD_DIM).transpose(0, 2, 1, 3)
        key = jax.random.key(seed)
        ks = jax.random.split(key, 12)
        B, S = (4, 1024)
        inp = {'query': jax.random.normal(ks[0], (B, S, HID), dtype=jnp.float32), 'key': jax.random.normal(ks[1], (B, S, HID), dtype=jnp.float32), 'value': jax.random.normal(ks[2], (B, S, HID), dtype=jnp.float32), 'mask': jax.random.randint(ks[3], (B, S, S), 0, 2, dtype=jnp.int32), 'Wq': jax.random.normal(ks[4], (HID, HID), dtype=jnp.float32) * (1.0 / np.sqrt(HID)), 'bq': jnp.zeros((HID,), dtype=jnp.float32), 'Wk': jax.random.normal(ks[5], (HID, HID), dtype=jnp.float32) * (1.0 / np.sqrt(HID)), 'bk': jnp.zeros((HID,), dtype=jnp.float32), 'Wv': jax.random.normal(ks[6], (HID, HID), dtype=jnp.float32) * (1.0 / np.sqrt(HID)), 'bv': jnp.zeros((HID,), dtype=jnp.float32), 'Wo': jax.random.normal(ks[7], (HID, HID), dtype=jnp.float32) * (1.0 / np.sqrt(HID)), 'bo': jnp.zeros((HID,), dtype=jnp.float32)}
        return inp
    _L0_xattn_all = _L0_xattn_setup()
    _L0_xattn_in = {k: v for k, v in _L0_xattn_all.items() if k in ('Wq', 'bq', 'Wk', 'bk', 'Wv', 'bv', 'Wo', 'bo')}
    del _L0_xattn_all

    def _L0_ffn_setup():
        import jax, jax.numpy as jnp
        import numpy as np
        FF_DIM = 1024
        TOP_K = 2
        key = jax.random.key(seed)
        k1, k2, k3, k4 = jax.random.split(key, 4)
        B, S, D, E, F = (2, 1024, 512, 8, FF_DIM)
        std = 0.006
        return {'x': jax.random.normal(k1, (B, S, D), dtype=jnp.float32), 'gate_w': jax.random.normal(k2, (D, E), dtype=jnp.float32) * 0.02, 'gate_up_w': jax.random.normal(k3, (E, D, 2 * F), dtype=jnp.float32) * std, 'down_w': jax.random.normal(k4, (E, F, D), dtype=jnp.float32) * std}
    _L0_ffn_all = _L0_ffn_setup()
    _L0_ffn_in = {k: v for k, v in _L0_ffn_all.items() if k in ('gate_w', 'gate_up_w', 'down_w')}
    del _L0_ffn_all
    return {'x': x, 'ctx_1024': ctx_1024, 'mask_BxSxS2_ik1': mask_BxSxS2_ik1, 'L0_attn_Wqkv': _L0_attn_in['Wqkv'], 'L0_attn_Wproj': _L0_attn_in['Wproj'], 'L0_attn_bproj': _L0_attn_in['bproj'], 'L0_xattn_Wq': _L0_xattn_in['Wq'], 'L0_xattn_bq': _L0_xattn_in['bq'], 'L0_xattn_Wk': _L0_xattn_in['Wk'], 'L0_xattn_bk': _L0_xattn_in['bk'], 'L0_xattn_Wv': _L0_xattn_in['Wv'], 'L0_xattn_bv': _L0_xattn_in['bv'], 'L0_xattn_Wo': _L0_xattn_in['Wo'], 'L0_xattn_bo': _L0_xattn_in['bo'], 'L0_ffn_gate_w': _L0_ffn_in['gate_w'], 'L0_ffn_gate_up_w': _L0_ffn_in['gate_up_w'], 'L0_ffn_down_w': _L0_ffn_in['down_w']}

def reference(x, ctx_1024, mask_BxSxS2_ik1, L0_attn_Wqkv, L0_attn_Wproj, L0_attn_bproj, L0_xattn_Wq, L0_xattn_bq, L0_xattn_Wk, L0_xattn_bk, L0_xattn_Wv, L0_xattn_bv, L0_xattn_Wo, L0_xattn_bo, L0_ffn_gate_w, L0_ffn_gate_up_w, L0_ffn_down_w):
    import jax
    import jax.numpy as jnp

    def _L0_attn_ref(x, Wqkv, Wproj, bproj):
        import jax, jax.numpy as jnp
        import numpy as np
        B, N, C, H, W = (2, 1024, 512, 16, 8)
        HD = C // H
        SCALE = HD ** (-0.5)

        def band_mask(n, w):
            i = jnp.arange(n)[:, None]
            j = jnp.arange(n)[None, :]
            lo = jnp.where(i <= w, 0, i - w)
            hi = jnp.where(n - i <= w, n - 1, i + w)
            return (j >= lo) & (j <= hi)
        b, n, c = x.shape
        qkv = (x @ Wqkv).reshape(b, n, 3, H, HD)
        qkv = jnp.transpose(qkv, (2, 0, 3, 1, 4))
        q, k, v = (qkv[0], qkv[1], qkv[2])
        attn = jnp.einsum('bhqd,bhkd->bhqk', q, k) * SCALE
        mask = band_mask(n, W)
        attn = jnp.where(mask[None, None], attn, jnp.float32(-1000000000.0))
        attn = jax.nn.softmax(attn, axis=-1)
        out = jnp.einsum('bhqk,bhkd->bhqd', attn, v)
        out = jnp.transpose(out, (0, 2, 1, 3)).reshape(b, n, c)
        return out @ Wproj + bproj

    def _L0_xattn_ref(query, key, value, mask, Wq, bq, Wk, bk, Wv, bv, Wo, bo):
        import jax, jax.numpy as jnp
        import numpy as np
        HID = 512
        HEADS = 16
        HEAD_DIM = HID // HEADS

        def _split_heads(x, W, b):
            B, S, _ = x.shape
            y = x @ W + b
            return y.reshape(B, S, HEADS, HEAD_DIM).transpose(0, 2, 1, 3)
        B, S, _ = query.shape
        Q = _split_heads(query, Wq, bq)
        K = _split_heads(key, Wk, bk)
        V = _split_heads(value, Wv, bv)
        scale = 1.0 / jnp.sqrt(jnp.asarray(HEAD_DIM, dtype=Q.dtype))
        energy = jnp.einsum('bhqd,bhkd->bhqk', Q, K) * scale
        m = mask[:, None, :, :]
        energy = jnp.where(m == 0, jnp.asarray(-1000000000.0, dtype=energy.dtype), energy)
        attn = jax.nn.softmax(energy, axis=-1)
        out = jnp.einsum('bhqk,bhkd->bhqd', attn, V)
        out = out.transpose(0, 2, 1, 3).reshape(B, S, HID)
        return out @ Wo + bo

    def _L0_ffn_ref(x, gate_w, gate_up_w, down_w):
        import jax, jax.numpy as jnp
        import numpy as np
        FF_DIM = 1024
        TOP_K = 2
        B, S, D = x.shape
        E = gate_up_w.shape[0]
        F = down_w.shape[1]
        x_flat = x.reshape(B * S, D)
        router_logits = x_flat @ gate_w
        router_probs = jax.nn.softmax(router_logits, axis=-1)
        top_k_probs, top_k_idx = jax.lax.top_k(router_probs, TOP_K)
        top_k_probs = top_k_probs / jnp.sum(top_k_probs, axis=-1, keepdims=True)
        gate_up = jnp.einsum('nd,edh->enh', x_flat, gate_up_w)
        gate_out = gate_up[..., :F]
        up_out = gate_up[..., F:]
        hidden = jax.nn.silu(gate_out) * up_out
        expert_out = jnp.einsum('enf,efd->end', hidden, down_w)
        out_t = jnp.transpose(expert_out, (1, 0, 2))
        sel = jnp.take_along_axis(out_t, top_k_idx[:, :, None], axis=1)
        output = jnp.sum(sel * top_k_probs[:, :, None], axis=1)
        return output.reshape(B, S, D)
    x = _layernorm(x + _L0_attn_ref(x, L0_attn_Wqkv, L0_attn_Wproj, L0_attn_bproj), axis=-1)
    x = _layernorm(x + _L0_xattn_ref(x, ctx_1024, ctx_1024, mask_BxSxS2_ik1, L0_xattn_Wq, L0_xattn_bq, L0_xattn_Wk, L0_xattn_bk, L0_xattn_Wv, L0_xattn_bv, L0_xattn_Wo, L0_xattn_bo), axis=-1)
    x = _layernorm(x + _L0_ffn_ref(x, L0_ffn_gate_w, L0_ffn_gate_up_w, L0_ffn_down_w), axis=-1)
    return x

_drawn_inputs = setup_inputs


def setup_inputs(seed=0):
    import zlib

    import numpy as np

    out = dict(_drawn_inputs(seed))
    spreads = {'L0_attn_bproj': (0.0, 0.1),
     'L0_xattn_bq': (0.0, 0.423),
     'L0_xattn_bk': (0.0, 0.8),
     'L0_xattn_bv': (0.0, 0.1),
     'L0_xattn_bo': (0.0, 0.1)}
    factors = {'L0_ffn_gate_w': 8.0, 'L0_ffn_gate_up_w': 8.0, 'L0_ffn_down_w': 8.0}
    for name, (base, spread) in spreads.items():
        noise = np.random.default_rng([zlib.crc32(name.encode()), seed]).standard_normal(out[name].shape)
        drawn = base * np.exp(spread * noise) if base else spread * noise
        out[name] = jnp.asarray(drawn.astype(out[name].dtype))
    for name, factor in factors.items():
        out[name] = (out[name] * factor).astype(out[name].dtype)
    return out
```

```python
from contextlib import ExitStack

import concourse.bass as bass
from concourse import mybir

ALU = mybir.AluOpType
ACT = mybir.ActivationFunctionType
AX_X = mybir.AxisListType.X
F32 = mybir.dt.float32
F32R = mybir.dt.float32r
I32 = mybir.dt.int32
U32 = mybir.dt.uint32

P = 128
MASKED = -float(2 ** 100)
LN_EPS = 1e-5


def make_constants(nc, S, T):
    B, N, C, QH = S["B"], S["N"], S["C"], S["QH"]
    with ExitStack() as ctx:
        zeroed = ctx.enter_context(nc.semaphore("zeroed"))
        made = ctx.enter_context(nc.semaphore("made"))
        rows_zeroed = ctx.enter_context(nc.semaphore("rows_zeroed"))
        loaded = ctx.enter_context(nc.semaphore("const_loaded"))
        block = ctx.enter_context(nc.Block())

        @block.sync
        def _(sp):
            sp.dma_start(T["wqkv"][:], S["Wqkv"].rearrange("(k p) n -> p k n", p=P)).then_inc(loaded, 16)
            sp.dma_start(T["wproj"][:], S["Wproj"].rearrange("(k p) n -> p k n", p=P)).then_inc(loaded, 16)
            sp.dma_start(T["resid"][:], S["x"].rearrange("b (h q) c -> q (b h) c", q=QH)).then_inc(loaded, 16)
            sp.dma_start(T["bias_row"][:], S["bproj"].rearrange("(a n) -> a n", a=1).broadcast_to([QH, C])).then_inc(loaded, 16)
            sp.wait_ge(zeroed, 3)
            sp.dma_start(S["x_rows"].rearrange("(t p) c -> p t c", p=P),
                         T["zeros"][:].rearrange("p (a c) -> p a c", a=1).broadcast_to([P, S["TILES"], C])).then_inc(rows_zeroed, 16)
            sp.wait_ge(loaded, 4 * 16)
            sp.wait_ge(rows_zeroed, 16)

        @block.gpsimd
        def _(pool):
            pool.memset(T["ident"][:], 0.0).then_inc(zeroed, 1)
            pool.memset(T["band"][:], 0.0).then_inc(zeroed, 1)
            pool.memset(T["zeros"][:], 0.0).then_inc(zeroed, 1)
            pool.wait_ge(zeroed, 3)
            pool.affine_select(out=T["ident"][:], in_=T["ident"][:], compare_op=ALU.not_equal, fill=1.0,
                               base=0, pattern=[[-1, P]], channel_multiplier=1).then_inc(made, 1)
            for h in range(2):
                off = h * (QH - S["KEY0"])
                b = T["band"][:, h, :]
                pool.affine_select(out=b, in_=b, compare_op=ALU.is_ge, fill=MASKED, base=S["W"] - off,
                                   pattern=[[1, S["KW"]]], channel_multiplier=-1).then_inc(made, 1)
                pool.wait_ge(made, 2 * h + 2)
                pool.affine_select(out=b, in_=b, compare_op=ALU.is_ge, fill=MASKED, base=S["W"] + off,
                                   pattern=[[-1, S["KW"]]], channel_multiplier=1).then_inc(made, 1)
            pool.wait_ge(made, 5)


def self_attention(nc, S, T):
    B, N, C, H, HD, QH, KW, KEY0 = (S[k] for k in ("B", "N", "C", "H", "HD", "QH", "KW", "KEY0"))
    KC = C // P
    J = P // HD
    UNITS = 2 * KC
    SCALE = HD ** -0.5
    with ExitStack() as ctx:
        def sb(name, shape, dt=F32):
            return ctx.enter_context(nc.sbuf_tensor(name, shape, dt))

        def sem(name):
            return ctx.enter_context(nc.semaphore(name))

        bank = [ctx.enter_context(nc.psum_tensor(f"a_bank{i}", [P, 512], F32)) for i in range(8)]
        score_bank, pt_bank, av_bank, proj_bank = bank[0:2], bank[2:4], bank[4:6], bank[6:8]

        x_tok = sb("a_x_tok", [QH, 2, C])
        xT = sb("a_xT", [P, KC, N])
        qk_hi = sb("a_qk_hi", [P, 2 * KC, N], F32R)
        qk_lo = sb("a_qk_lo", [P, 2 * KC, N], F32R)
        q_stack = sb("a_q_stack", [P, J, KC, N], F32R)
        k_stack = sb("a_k_stack", [P, J, KC, N], F32R)
        v_tok = [sb(f"a_v_tok{i}", [KW, 2, C]) for i in range(2)]
        probs = sb("a_probs", [QH, UNITS, J, KW])
        row_max = sb("a_row_max", [QH, UNITS, J])
        neg_max = sb("a_neg_max", [QH, UNITS, J])
        row_sum = sb("a_row_sum", [QH, UNITS, J])
        inv_sum = sb("a_inv_sum", [QH, UNITS, J])
        probsT = [sb(f"a_probsT{i}", [KW, J, QH]) for i in range(2)]
        attnT = [sb(f"a_attnT{i}", [P, KC, QH]) for i in range(2)]
        waited = sb("a_waited", [QH, 1])

        x_loaded = sem("x_loaded")
        xT_in_psum = sem("xT_in_psum")
        xT_ready = sem("xT_ready")
        qk_in_psum = sem("qk_in_psum")
        qk_hi_ready = sem("qk_hi_ready")
        qk_lo_ready = sem("qk_lo_ready")
        v_in_psum = sem("v_in_psum")
        v_ready = sem("v_ready")
        q_stacked = sem("q_stacked")
        k_stacked = sem("k_stacked")
        scores_in_psum = sem("scores_in_psum")
        masked_ready = sem("masked_ready")
        max_ready = sem("max_ready")
        exp_ready = sem("exp_ready")
        inv_ready = sem("inv_ready")
        probs_ready = sem("probs_ready")
        pT_in_psum = sem("pT_in_psum")
        pT_ready = sem("pT_ready")
        av_in_psum = sem("av_in_psum")
        attnT_ready = sem("attnT_ready")
        out_in_psum = sem("out_in_psum")
        out_added = sem("out_added")
        bias_added = sem("bias_added")

        block = ctx.enter_context(nc.Block())

        def steps(eng, step):
            with eng.Fori(0, B // 2 - 1) as pair:
                step(pair * 2, 0)
                step(pair * 2 + 1, 1)
            step(B - 2, 0)
            step(B - 1, 1, last=True)

        @block.sync
        def _(sp):
            def load_x(b):
                sp.dma_start(x_tok[:], S["x"].rearrange("b (h q) c -> b q h c", q=QH)[bass.ds(b, 1)].rearrange("a q h c -> (a q) h c")).then_inc(x_loaded, 16)

            def stack(b):
                sp.wait_ge(qk_hi_ready, b * 8 + 8)
                sp.wait_ge(qk_lo_ready, b * 8 + 8)
                for dst, first, order, done in ((q_stack, 0, (qk_hi, qk_hi, qk_lo, qk_lo), q_stacked),
                                                (k_stack, KC, (qk_hi, qk_lo, qk_hi, qk_lo), k_stacked)):
                    for g, src in enumerate(order):
                        for j in range(J):
                            sp.dma_start(dst[HD * g:HD * g + HD, j].bitcast(F32), src[HD * j:HD * j + HD, first:first + KC].bitcast(F32)).then_inc(done, 16)

            def step(b, par, last=False):
                if last:
                    return
                sp.wait_ge(scores_in_psum, b * 8 + 8)
                stack(b + 1)
                if not (isinstance(b, int) and b == B - 2):
                    load_x(b + 2)
            load_x(0)
            sp.wait_ge(xT_in_psum, 2)
            stack(0)
            load_x(1)
            steps(sp, step)

        @block.tensor
        def _(pe):
            def transposes(b, par):
                pe.wait_ge(x_loaded, b * 16 + 16)
                for h in range(2):
                    if not (isinstance(b, int) and b == 0):
                        pe.wait_ge(v_ready, b * 2 - 1 + h)
                        pe.wait_ge(out_added, b * 2 - 1 + h)
                    for k in range(KC):
                        last = pe.transpose(proj_bank[h][:, k * QH:(k + 1) * QH], x_tok[:, h, k * P:(k + 1) * P],
                                            T["ident"][0:QH, 0:QH])
                    last.then_inc(xT_in_psum, 1)

            def project_qk(b, n):
                if n < 2:
                    pe.wait_ge(xT_ready, b * 2 + 2)
                else:
                    pe.wait_ge(qk_lo_ready, b * 8 + n - 1)
                for k in range(KC):
                    last = pe.matmul(proj_bank[n % 2][:, 0:N], T["wqkv"][:, k, n * P:(n + 1) * P], xT[:, k, :],
                                     start=(k == 0), stop=(k == KC - 1))
                last.then_inc(qk_in_psum, 1)

            def project_v(b, w):
                pe.wait_ge(qk_lo_ready, b * 8 + 7 + w)
                for k in range(KC):
                    last = pe.matmul(proj_bank[w][0:KW, :], xT[:, k, KEY0 * w:KEY0 * w + KW], T["wqkv"][:, k, 2 * C:3 * C],
                                     start=(k == 0), stop=(k == KC - 1))
                last.then_inc(v_in_psum, 1)

            def scores(b, u):
                h, c = divmod(u, KC)
                if u == 0:
                    pe.wait_ge(q_stacked, b * 256 + 256)
                    pe.wait_ge(k_stacked, b * 256 + 256)
                if u >= 2:
                    pe.wait_ge(masked_ready, b * 8 + u - 1)
                for j in range(J):
                    last = pe.matmul(score_bank[u % 2][0:QH, j * KW:(j + 1) * KW], q_stack[:, j, c, h * QH:(h + 1) * QH],
                                     k_stack[:, j, c, KEY0 * h:KEY0 * h + KW], start=True, stop=True)
                last.then_inc(scores_in_psum, 1)

            def turn_probs(b, u):
                pe.wait_ge(probs_ready, b * 8 + u + 1)
                if u >= 2:
                    pe.wait_ge(pT_ready, b * 8 + u - 1)
                for j in range(J):
                    last = pe.transpose(pt_bank[u % 2][0:KW, j * QH:(j + 1) * QH], probs[:, u, j, :], T["ident"][0:QH, 0:QH])
                last.then_inc(pT_in_psum, 1)

            def weigh_values(b, u, par):
                h, c = divmod(u, KC)
                pe.wait_ge(pT_ready, b * 8 + u + 1)
                if u == 0:
                    pe.wait_ge(v_ready, b * 2 + 2)
                for j in range(J):
                    last = pe.matmul(av_bank[h][HD * j:HD * (j + 1), c * QH:(c + 1) * QH],
                                     v_tok[par][:, h, P * c + HD * j:P * c + HD * (j + 1)], probsT[u % 2][:, j, :],
                                     start=True, stop=True)
                last.then_inc(av_in_psum, 1)

            def project_out(b, h, last):
                pe.wait_ge(attnT_ready, b * 2 + h + 1)
                if last:
                    pe.wait_ge(out_added, b * 2 + 1 + h)
                else:
                    pe.wait_ge(v_ready, b * 2 + 3 + h)
                for c in range(KC):
                    mm = pe.matmul(proj_bank[h][0:QH, :], attnT[h][:, c, :], T["wproj"][:, c, :],
                                   start=(c == 0), stop=(c == KC - 1))
                mm.then_inc(out_in_psum, 1)

            def step(b, par, last=False):
                if not last:
                    transposes(b + 1, 1 - par)
                for u in range(UNITS):
                    scores(b, u)
                    if not last:
                        project_qk(b + 1, u)
                if not last:
                    project_v(b + 1, 0)
                    project_v(b + 1, 1)
                turn_probs(b, 0)
                for u in range(1, UNITS):
                    turn_probs(b, u)
                    weigh_values(b, u - 1, par)
                weigh_values(b, UNITS - 1, par)
                for h in range(2):
                    project_out(b, h, last)

            transposes(0, 0)
            for n in range(2 * KC):
                project_qk(0, n)
            project_v(0, 0)
            project_v(0, 1)
            steps(pe, step)

        @block.scalar
        def _(act):
            def turn_x(b):
                for h in range(2):
                    act.wait_ge(xT_in_psum, b * 2 + h + 1)
                    act.activation(xT[:, :, h * QH:(h + 1) * QH],
                                   proj_bank[h][:, 0:KC * QH].rearrange("p (k q) -> p k q", k=KC), ACT.Copy).then_inc(xT_ready, 1)

            def high(b, n):
                act.wait_ge(qk_in_psum, b * 8 + n + 1)
                if n == 0 and not (isinstance(b, int) and b == 0):
                    act.wait_ge(q_stacked, b * 256)
                    act.wait_ge(k_stacked, b * 256)
                act.activation(qk_hi[:, n, :], proj_bank[n % 2][:, 0:N], ACT.Copy).then_inc(qk_hi_ready, 1)

            def values(b, par):
                for w in range(2):
                    act.wait_ge(v_in_psum, b * 2 + w + 1)
                    act.activation(v_tok[par][:, w, :], proj_bank[w][0:KW, :], ACT.Copy).then_inc(v_ready, 1)

            def exps(b, u):
                act.wait_ge(max_ready, b * 8 + u + 1)
                for j in range(J):
                    last = act.activation(probs[:, u, j, :], probs[:, u, j, :], ACT.Exp, bias=neg_max[:, u, j:j + 1],
                                          scale=SCALE, accum_out=row_sum[:, u, j:j + 1])
                last.then_inc(exp_ready, 1)

            def attn_out(b, h):
                act.wait_ge(av_in_psum, b * 8 + KC * h + KC)
                act.wait_ge(out_added, b * 2 + 1 + h)
                act.activation(attnT[h][:], av_bank[h][:, 0:KC * QH].rearrange("p (k q) -> p k q", k=KC), ACT.Copy).then_inc(attnT_ready, 1)

            def step(b, par, last=False):
                if not last:
                    turn_x(b + 1)
                for u in range(UNITS):
                    if not last:
                        high(b + 1, u)
                    exps(b, u)
                if not last:
                    values(b + 1, 1 - par)
                for h in range(2):
                    attn_out(b, h)

            turn_x(0)
            for n in range(2 * KC):
                high(0, n)
            values(0, 0)
            steps(act, step)

        @block.vector
        def _(dve):
            def low(b, n):
                dve.wait_ge(qk_hi_ready, b * 8 + n + 1)
                dve.tensor_tensor(qk_lo[:, n, :], proj_bank[n % 2][:, 0:N], qk_hi[:, n, :], ALU.subtract).then_inc(qk_lo_ready, 1)

            def mask_and_max(b, u):
                h = u // KC
                for j in range(J):
                    last = dve.tensor_tensor_reduce(probs[:, u, j, :], score_bank[u % 2][0:QH, j * KW:(j + 1) * KW],
                                                    T["band"][:, h, :], 1.0, MASKED, ALU.add, ALU.max, row_max[:, u, j:j + 1])
                last.then_inc(masked_ready, 1)
                dve.wait_ge(masked_ready, b * 8 + u + 1)
                dve.tensor_scalar(neg_max[:, u, :], row_max[:, u, :], -SCALE, None, ALU.mult).then_inc(max_ready, 1)

            def invert(b, u):
                dve.wait_ge(exp_ready, b * 8 + u + 1)
                dve.reciprocal(inv_sum[:, u, :], row_sum[:, u, :]).then_inc(inv_ready, 1)

            def copy_pT(b, u):
                dve.wait_ge(pT_in_psum, b * 8 + u + 1)
                if u >= 2:
                    dve.wait_ge(av_in_psum, b * 8 + u - 1)
                dve.tensor_copy(probsT[u % 2][:].rearrange("k j q -> k (j q)"), pt_bank[u % 2][0:KW, 0:J * QH]).then_inc(pT_ready, 1)

            def add_out(b, h):
                dve.wait_ge(out_in_psum, b * 2 + h + 1)
                r = T["resid"][:, bass.ds(b * 2 + h, 1), :].rearrange("q a c -> q (a c)")
                dve.tensor_tensor(r, proj_bank[h][0:QH, :], r, ALU.add).then_inc(out_added, 1)
                dve.wait_ge(out_added, b * 2 + h + 3)
                dve.memset(waited[:], 0.0)
                dve.bn_stats(T["stats"][:, bass.ds(b * 2 + h, 1), :].rearrange("q a c -> q (a c)"), r)

            def step(b, par, last=False):
                for u in range(UNITS):
                    dve.wait_ge(scores_in_psum, b * 8 + u + 1)
                    if not last:
                        low(b + 1, u)
                    mask_and_max(b, u)
                    if u >= 1:
                        invert(b, u - 1)
                invert(b, UNITS - 1)
                for u in range(UNITS):
                    copy_pT(b, u)
                for h in range(2):
                    add_out(b, h)

            dve.memset(waited[:], 0.0).then_inc(out_added, 2)
            dve.wait_ge(bias_added, 1)
            for n in range(2 * KC):
                low(0, n)
            steps(dve, step)

        @block.gpsimd
        def _(pool):
            pool.tensor_tensor(T["resid"][:], T["resid"][:], T["bias_row"][:].rearrange("q (a c) -> q a c", a=1).broadcast_to([QH, 2 * B, C]), ALU.add).then_inc(bias_added, 1)

            def step(b, par, last=False):
                for u in range(UNITS):
                    pool.wait_ge(inv_ready, b * 8 + u + 1)
                    pool.tensor_tensor(probs[:, u], probs[:, u],
                                       inv_sum[:, u].rearrange("q (j a) -> q j a", a=1).broadcast_to([QH, J, KW]), ALU.mult).then_inc(probs_ready, 1)
            steps(pool, step)


def normalise_and_turn(nc, S, T, name, bias=None, router=False):
    B, N, C, QH = S["B"], S["N"], S["C"], S["QH"]
    KC = C // P
    ROWS = 2 * B
    with ExitStack() as ctx:
        def sb(n, shape, dt=F32):
            return ctx.enter_context(nc.sbuf_tensor(f"{name}_{n}", shape, dt))

        def sem(n):
            return ctx.enter_context(nc.semaphore(f"{name}_{n}"))

        turn_bank = [ctx.enter_context(nc.psum_tensor(f"{name}_bank{i}", [P, 512], F32)) for i in range(2)]
        if router:
            gate_w = sb("gate_w", [P, KC, S["E"]])
            logit_bank = ctx.enter_context(nc.psum_tensor(f"{name}_logits", [P, ROWS, S["E"]], F32))
        x_norm = [sb(f"x_norm{i}", [QH, C]) for i in range(2)]
        xT_tile = [sb(f"xT_tile{i}", [P, KC, QH]) for i in range(2)]
        std = sb("std", [QH, ROWS])
        rstd = sb("rstd", [QH, ROWS])
        eps = sb("eps", [QH, 1])
        mean_var, stats = T["mean_var"], T["stats"]

        bias_loaded = sem("bias_loaded")
        eps_set = sem("eps_set")
        var_ready = sem("var_ready")
        std_ready = sem("std_ready")
        rstd_ready = sem("rstd_ready")
        logits_in_psum = sem("logits_in_psum")
        norm_ready = sem("norm_ready")
        turned = sem("turned")
        xT_copied = sem("xT_copied")
        xT_stored = sem("xT_stored")
        tiles_free = sem("tiles_free")
        resid_set = sem("resid_set")
        block = ctx.enter_context(nc.Block())

        @block.sync
        def _(sp):
            for freed in (turned, xT_copied, resid_set, tiles_free):
                sp.sem_inc(freed, 2)
            if router:
                sp.dma_start(gate_w[:], S["gate_w"].rearrange("(k p) e -> p k e", p=P)).then_inc(bias_loaded, 16)
                return
            sp.dma_start(T["bias_row"][:], bias.rearrange("(a n) -> a n", a=1).broadcast_to([QH, C])).then_inc(bias_loaded, 16)
            with sp.Fori(0, ROWS // 2) as pair:
                for i in range(2):
                    r = pair * 2 + i
                    sp.wait_ge(xT_copied, r + 3)
                    sp.dma_start(S["xT"][bass.ds(r, 1)].rearrange("a p k q -> (a p) k q"), xT_tile[i][:]).then_inc(xT_stored, 16)
                sp.wait_ge(xT_stored, pair * 32 + 32)
                sp.sem_inc(tiles_free, 2)

        @block.vector
        def _(dve):
            dve.memset(eps[:], LN_EPS).then_inc(eps_set, 1)
            for r in range(ROWS):
                last = dve.bn_aggr(mean_var[:, r, :], stats[:, r, :])
            last.then_inc(var_ready, 1)
            dve.wait_ge(std_ready, 1)
            dve.reciprocal(rstd[:], std[:]).then_inc(rstd_ready, 1)
            dve.wait_ge(rstd_ready, 1)
            dve.tensor_copy(mean_var[:, :, 1], rstd[:]).then_inc(rstd_ready, 1)
            dve.wait_ge(rstd_ready, 2)
            with dve.Fori(0, ROWS // 2) as pair:
                for i in range(2):
                    r = pair * 2 + i
                    dve.wait_ge(turned, r + 1)
                    dve.wait_ge(resid_set, r + 1)
                    dve.tensor_scalar(x_norm[i][:], T["resid"][:, bass.ds(r, 1), :].rearrange("q a c -> q (a c)"),
                                      mean_var[:, bass.ds(r, 1), 0], mean_var[:, bass.ds(r, 1), 1],
                                      ALU.subtract, ALU.mult).then_inc(norm_ready, 1)
            if router:
                dve.wait_ge(logits_in_psum, ROWS)
                dve.tensor_copy(T["logits"][:], logit_bank[0:QH])

        @block.scalar
        def _(act):
            act.wait_ge(eps_set, 1)
            act.wait_ge(var_ready, 1)
            act.activation(std[:], mean_var[:, :, 1], ACT.Sqrt, bias=eps[:]).then_inc(std_ready, 1)
            with act.Fori(0, ROWS // 2) as pair:
                for i in range(2):
                    r = pair * 2 + i
                    act.wait_ge(turned, r + 3)
                    if i == 0 and not router:
                        act.wait_ge(tiles_free, pair * 2 + 2)
                    act.activation(xT_tile[i][:],
                                   turn_bank[i][:, 0:KC * QH].rearrange("p (k q) -> p k q", k=KC), ACT.Copy).then_inc(xT_copied, 1)

        @block.tensor
        def _(pe):
            if router:
                pe.wait_ge(bias_loaded, 16)
            with pe.Fori(0, ROWS // 2) as pair:
                for i in range(2):
                    r = pair * 2 + i
                    pe.wait_ge(norm_ready, r + 1)
                    pe.wait_ge(xT_copied, r + 1)
                    for k in range(KC):
                        last = pe.transpose(turn_bank[i][:, k * QH:(k + 1) * QH], x_norm[i][:, k * P:(k + 1) * P], T["ident"][0:QH, 0:QH])
                    last.then_inc(turned, 1)
                    if router:
                        pe.wait_ge(xT_copied, r + 3)
                        for k in range(KC):
                            mm = pe.matmul(logit_bank[0:QH, bass.ds(r, 1), :].rearrange("q a e -> q (a e)"), xT_tile[i][:, k, :], gate_w[:, k, :],
                                           start=(k == 0), stop=(k == KC - 1))
                        mm.then_inc(logits_in_psum, 1)

        @block.gpsimd
        def _(pool):
            if not router:
                pool.wait_ge(bias_loaded, 16)
            with pool.Fori(0, ROWS // 2) as pair:
                for i in range(2):
                    r = pair * 2 + i
                    pool.wait_ge(norm_ready, r + 1)
                    row = T["resid"][:, bass.ds(r, 1), :].rearrange("q a c -> q (a c)")
                    if router:
                        pool.tensor_copy(row, x_norm[i][:]).then_inc(resid_set, 1)
                    else:
                        pool.tensor_tensor(row, x_norm[i][:], T["bias_row"][:], ALU.add).then_inc(resid_set, 1)


class Uses:

    def __init__(self, B):
        self.prologue = [("ctx", t) for t in range(6)] + ["k0", "k1", "q"] + [("v", t) for t in range(3)]
        self.kinds = {k: self.batch(k) for k in ("first", "mid", "last")}
        self.B = B
        self.tail = [("out", 0), ("out", 1)]

    @staticmethod
    def chunk(kind, c):
        uses = []
        if c == 3 and kind != "last":
            uses += [("ctx", t) for t in range(6)]
        if not (c == 3 and kind == "last"):
            uses += ["k0", "k1", "q"]
        uses.append("m")
        if c == 0:
            uses += [("v", t) for t in range(3, 6)]
        if c in (1, 2) and kind != "first":
            uses.append(("out", c - 1))
        if c == 3 and kind != "last":
            uses += [("v", t) for t in range(3)]
        return uses

    def batch(self, kind):
        return [(c, u) for c in range(4) for u in self.chunk(kind, c)]

    def find(self, b, kind, c, what):
        if kind == "prologue":
            i = self.prologue.index(what)
            return i % 2, i // 2 + 1
        first = len(self.prologue)
        if kind == "tail":
            i = first + len(self.kinds["first"]) + (self.B - 2) * len(self.kinds["mid"]) + len(self.kinds["last"]) + what
            return i % 2, i // 2 + 1
        i = self.kinds[kind].index((c, what))
        if kind == "first":
            i += first
            return i % 2, i // 2 + 1
        a, m = first + len(self.kinds["first"]), len(self.kinds["mid"])
        assert a % 2 == 0 and m % 2 == 0
        return i % 2, (b - 1) * (m // 2) + (a // 2 + i // 2 + 1)


def cross_attention(nc, S, T):
    B, N, C, HD, QH = (S[k] for k in ("B", "N", "C", "HD", "QH"))
    NK = S["ctx"].shape[1]
    KC = C // P
    J = P // HD
    KT = 6
    KR = NK // KT
    KH = 376
    KP = 2 * KH
    HALF = NK // 2
    R3 = 3 * HD
    SCALE = HD ** -0.5
    uses = Uses(B)
    with ExitStack() as ctx:
        def sb(name, shape, dt=F32):
            return ctx.enter_context(nc.sbuf_tensor(f"b_{name}", shape, dt))

        def sem(name):
            return ctx.enter_context(nc.semaphore(f"b_{name}"))

        ring = ctx.enter_context(nc.psum_tensor("b_ring", [P, 4, 512], F32))
        av_bank = [ctx.enter_context(nc.psum_tensor(f"b_av{i}", [P, 512], F32)) for i in range(2)]
        proj_bank = [ctx.enter_context(nc.psum_tensor(f"b_proj{i}", [P, 512], F32)) for i in range(2)]

        wq, wk, wv, wo = (sb(n, [P, KC, C]) for n in ("wq", "wk", "wv", "wo"))
        bq_col, bk_col = sb("bq_col", [P, KC]), sb("bk_col", [P, KC])
        bv_row = sb("bv_row", [P, C])
        ones = sb("ones", [P, HD])
        ident_r = sb("ident_r", [P, P], F32R)
        ctx_tok = [sb(f"ctx_tok{i}", [KR, C]) for i in range(2)]
        ctxT = sb("ctxT", [P, KC, NK])
        k_hi, k_lo = sb("k_hi", [P, NK], F32R), sb("k_lo", [P, NK], F32R)
        q_hi, q_lo = sb("q_hi", [P, N], F32R), sb("q_lo", [P, N], F32R)
        k_stack = [sb(f"k_stack{i}", [P, J, KP], F32R) for i in range(2)]
        q_stack = [sb(f"q_stack{i}", [P, J, N], F32R) for i in range(2)]
        xT = [sb(f"xT{i}", [P, 2, KC, QH]) for i in range(2)]
        mask_int = sb("mask_int", [QH, 2, NK], I32)
        mask_bias = [sb(f"mask_bias{i}", [QH, 2, KP], F32R) for i in range(2)]
        row_max = [sb(f"row_max{i}", [QH, J * 2]) for i in range(2)]
        neg_max = sb("neg_max", [QH, J * 2], F32R)
        neg_max_rows = sb("neg_max_rows", [J * 2, QH])
        v_tok = [sb(f"v_tok{i}", [KR, KT, C]) for i in range(2)]
        probsT = [sb(f"probsT{i}", [KR, KT, N]) for i in range(2)]
        half_sum = sb("half_sum", [KR, 3, N])
        key_sum = [sb(f"key_sum{i}", [KR, N]) for i in range(2)]
        inv_den = sb("inv_den", [P, N])
        attnT = [sb(f"attnT{i}", [P, KC, N]) for i in range(2)]
        waited = sb("waited", [QH, 5])

        w_loaded = sem("w_loaded")
        set_up = sem("set_up")
        ctx_loaded = [sem(f"ctx_loaded{i}") for i in range(2)]
        xT_loaded = sem("xT_loaded")
        mask_loaded = sem("mask_loaded")
        mask_ready = sem("mask_ready")
        filled = [sem(f"filled{i}") for i in range(2)]
        freed = [sem(f"freed{i}") for i in range(2)]
        hi_ready = sem("hi_ready")
        stacked = [sem(f"stacked{j}") for j in range(J)]
        s_in_psum = sem("s_in_psum")
        max_ready = sem("max_ready")
        neg_ready = sem("neg_ready")
        max_placed = sem("max_placed")
        st_in_psum = sem("st_in_psum")
        exp_ready = sem("exp_ready")
        av_in_psum = sem("av_in_psum")
        halves_added = sem("halves_added")
        sum_ready = sem("sum_ready")
        den_in_psum = sem("den_in_psum")
        inv_ready = sem("inv_ready")
        attnT_ready = sem("attnT_ready")

        block = ctx.enter_context(nc.Block())

        def steps(eng, chunk):
            def batch(b, kind, par):
                for c in range(KC):
                    if c < KC - 1:
                        after = (b, c + 1, par)
                    else:
                        after = (b + 1, 0, 1 - par) if kind != "last" else None
                    chunk(b, c, kind, par, after)
            batch(0, "first", 0)
            with eng.Fori(0, B // 2 - 1) as pair:
                batch(pair * 2 + 1, "mid", 1)
                batch(pair * 2 + 2, "mid", 0)
            batch(B - 1, "last", 1)

        def wait_free(pe, b, kind, c, what):
            i, n = uses.find(b, kind, c, what)
            if not (isinstance(n, int) and n == 1):
                pe.wait_ge(freed[i], n - 1)
            return i

        def wait_filled(eng, b, kind, c, what):
            i, n = uses.find(b, kind, c, what)
            eng.wait_ge(filled[i], n)
            return i

        def wait_freed(eng, b, kind, c, whats):
            for what in whats:
                i, n = uses.find(b, kind, c, what)
                eng.wait_ge(freed[i], n)

        @block.sync
        def _(sp):
            def load_ctx(b, t):
                sp.dma_start(ctx_tok[t % 2][:], S["ctx"].rearrange("b (t p) c -> b t p c", p=KR)[bass.ds(b, 1), t].rearrange("a p c -> (a p) c")).then_inc(ctx_loaded[t % 2], 16)

            def load_xT(b, par):
                sp.dma_start(xT[par][:].rearrange("p h k q -> p h (k q)"),
                             S["xT"].rearrange("(b h) p k q -> b p h (k q)", h=2)[bass.ds(b, 1)].rearrange("a p h n -> (a p) h n")).then_inc(xT_loaded, 16)

            def load_mask(b):
                sp.dma_start(mask_int[:], S["mask"].rearrange("b (h q) k -> b q h k", q=QH)[bass.ds(b, 1)].rearrange("a q h k -> (a q) h k")).then_inc(mask_loaded, 16)

            def stack(i, kind, c, bk):
                wait_freed(sp, bk, kind, c, ("k1", "q"))
                for j in range(J):
                    for dst, order, n in ((q_stack, (q_hi, q_hi, q_lo), N), (k_stack, (k_hi, k_lo, k_hi), NK)):
                        for r, src in enumerate(order):
                            sp.dma_start(dst[i][HD * r:HD * r + HD, j, 0:n].bitcast(F32),
                                         src[HD * j:HD * j + HD, :].bitcast(F32)).then_inc(stacked[j], 16)

            def chunk(b, c, kind, par, after):
                g = b * KC + c
                wait_freed(sp, b, kind, c, ("m",))
                sp.dma_start(q_stack[c % 2][R3:R3 + 1, :, :].bitcast(F32).rearrange("a j (h q) -> a (j h) q", h=2),
                             neg_max_rows[:]).then_inc(max_placed, 16)
                if after is not None:
                    stack(after[1] % 2, kind, c, b)
                if kind != "last":
                    if c == 1:
                        sp.wait_ge(mask_ready, b + 1)
                        load_mask(b + 1)
                        load_xT(b + 1, 1 - par)
                    if c == 2:
                        load_ctx(b + 1, 0)
                        load_ctx(b + 1, 1)
                    if c == 3:
                        pass

            def chunk_with_ctx(b, c, kind, par, after):
                if c == 3 and kind != "last":
                    for t in range(2, KT):
                        wait_filled(sp, b, kind, c, ("ctx", t - 2))
                        load_ctx(b + 1, t)
                chunk(b, c, kind, par, after)

            for dst, name in ((wk, "Wk"), (wv, "Wv"), (wq, "Wq"), (wo, "Wo")):
                sp.dma_start(dst[:], S[name].rearrange("(k p) n -> p k n", p=P)).then_inc(w_loaded, 16)
            sp.dma_start(bv_row[:], S["bv"].rearrange("(a n) -> a n", a=1).broadcast_to([P, C])).then_inc(w_loaded, 16)
            for dst, name in ((bq_col, "bq"), (bk_col, "bk")):
                with nc.allow_non_contiguous_dma(reason="two columns of 4 x 128 values"):
                    sp.dma_start(dst[:], S[name].rearrange("(k p) -> p k", p=P)).then_inc(w_loaded, 16)
            load_mask(0)
            load_xT(0, 0)
            for t in range(KT):
                if t >= 2:
                    wait_filled(sp, 0, "prologue", 0, ("ctx", t - 2))
                load_ctx(0, t)
            stack(0, "prologue", 0, 0)
            steps(sp, chunk_with_ctx)

        @block.tensor
        def _(pe):
            def turn_ctx(b, kind, c, t, bk):
                i = wait_free(pe, bk, kind, c, ("ctx", t))
                pe.wait_ge(ctx_loaded[t % 2], (b * (KT // 2) + t // 2) * 16 + 16)
                for k in range(KC):
                    mm = pe.transpose(proj_bank[i][:, k * KR:(k + 1) * KR], ctx_tok[t % 2][:, k * P:(k + 1) * P], T["ident"][0:KR, 0:KR])
                mm.then_inc(filled[i], 1)

            def project_k(b, cn, kind, c, half, bk):
                i = wait_free(pe, bk, kind, c, f"k{half}")
                if half == 0 and cn == 0:
                    wait_freed(pe, bk, kind, c, (("ctx", KT - 2), ("ctx", KT - 1)))
                for k in range(KC):
                    mm = pe.matmul(proj_bank[i][:, 0:HALF], wk[:, k, cn * P:(cn + 1) * P], ctxT[:, k, half * HALF:(half + 1) * HALF],
                                   start=(k == 0), stop=(k == KC - 1))
                mm.then_inc(filled[i], 1)

            def project_q(b, cn, kind, c, bk, xpar):
                i = wait_free(pe, bk, kind, c, "q")
                if cn == 0:
                    pe.wait_ge(xT_loaded, b * 16 + 16)
                for k in range(KC):
                    mm = pe.matmul(proj_bank[i][:, 0:N], wq[:, k, cn * P:(cn + 1) * P], xT[xpar][:, :, k, :],
                                   start=(k == 0), stop=(k == KC - 1))
                mm.then_inc(filled[i], 1)

            def project_v(b, kind, c, t, bk):
                i = wait_free(pe, bk, kind, c, ("v", t))
                for k in range(KC):
                    mm = pe.matmul(proj_bank[i][0:KR, :], ctxT[:, k, t * KR:(t + 1) * KR], wv[:, k, :],
                                   start=(k == 0), stop=(k == KC - 1))
                mm.then_inc(filled[i], 1)

            def project_out(b, h, kind, c, what, par, bk):
                i = wait_free(pe, bk, kind, c, what)
                if h == 0:
                    pe.wait_ge(attnT_ready, b * KC + KC)
                for k in range(KC):
                    mm = pe.matmul(proj_bank[i][0:QH, :], attnT[par][:, k, h * QH:(h + 1) * QH], wo[:, k, :],
                                   start=(k == 0), stop=(k == KC - 1))
                mm.then_inc(filled[i], 1)

            def turn_max(b, kind, c):
                i = wait_free(pe, b, kind, c, "m")
                pe.wait_ge(neg_ready, b * KC + c + 1)
                pe.transpose(proj_bank[i][0:J * 2, 0:QH], neg_max[:].bitcast(F32), T["ident"][0:QH, 0:QH]).then_inc(filled[i], 1)

            def scores(b, c, u, prologue=False):
                g = b * KC + c
                j, h = divmod(u, 2)
                if h == 0:
                    pe.wait_ge(stacked[j], g * 96 + 96)
                if u < 2:
                    if not prologue:
                        pe.wait_ge(exp_ready, g * 12 - 2 + 2 * u)
                else:
                    pe.wait_ge(max_ready, g * 8 + u - 1)
                for a in range(2):
                    mm = pe.matmul(ring[0:QH, 2 * (u % 2) + a, 0:KH], q_stack[c % 2][0:R3, j, h * QH:(h + 1) * QH],
                                   k_stack[c % 2][0:R3, j, a * KH:(a + 1) * KH], start=True, stop=True)
                mm.then_inc(s_in_psum, 1)

            def scoresT(b, c, j, par):
                g = b * KC + c
                for r in range(3 * j, 3 * j + 3):
                    if r == 0:
                        pe.wait_ge(max_placed, g * 16 + 16)
                    if r < 4:
                        if r == 0:
                            pe.wait_ge(max_ready, g * 8 + 8)
                    else:
                        pe.wait_ge(exp_ready, g * 12 + r - 3)
                    for a in range(2):
                        t = 2 * (r % 3) + a
                        out = ring[0:KR, r % 4, a * N:(a + 1) * N]
                        pe.matmul(out, k_stack[c % 2][:, j, t * KR:(t + 1) * KR], q_stack[c % 2][:, j, :], start=True, stop=False)
                        for h in range(2):
                            mm = pe.matmul(ring[0:KR, r % 4, a * N + h * QH:a * N + (h + 1) * QH],
                                           mask_bias[par][:, h, t * KR:(t + 1) * KR], ident_r[0:QH, 0:QH], start=False, stop=(h == 1))
                    mm.then_inc(st_in_psum, 1)

            def weigh_values(b, c, j, par, kind):
                g = b * KC + c
                pe.wait_ge(exp_ready, g * 12 + 3 * j + 3)
                if c == 0 and j == 0:
                    wait_freed(pe, b, kind, c, (("v", KT - 2), ("v", KT - 1)))
                for t in range(KT):
                    mm = pe.matmul(av_bank[c % 2][HD * j:HD * (j + 1), 0:N], v_tok[par][:, t, P * c + HD * j:P * c + HD * (j + 1)],
                                   probsT[j % 2][:, t, :], start=(t == 0), stop=(t == KT - 1))
                mm.then_inc(av_in_psum, 1)

            def sum_probs(b, c, j):
                pe.wait_ge(sum_ready, (b * KC + c) * J + j + 1)
                pe.matmul(av_bank[c % 2][HD * j:HD * (j + 1), 256:256 + N], ones[0:KR, :], key_sum[j % 2][:],
                          start=True, stop=True).then_inc(den_in_psum, 1)

            def chunk(b, c, kind, par, after):
                if c == 3 and kind != "last":
                    for t in range(KT):
                        turn_ctx(b + 1, kind, c, t, b)
                if after is not None:
                    project_k(after[0], after[1], kind, c, 0, b)
                    project_k(after[0], after[1], kind, c, 1, b)
                    project_q(after[0], after[1], kind, c, b, after[2])
                turn_max(b, kind, c)
                if c == 0:
                    for t in range(3, KT):
                        project_v(b, kind, c, t, b)
                if c in (1, 2) and kind != "first":
                    project_out(b - 1, c - 1, kind, c, ("out", c - 1), 1 - par, b)
                if c == 3 and kind != "last":
                    for t in range(3):
                        project_v(b + 1, kind, c, t, b)
                for j in range(J):
                    scoresT(b, c, j, par)
                    if j >= 1:
                        weigh_values(b, c, j - 1, par, kind)
                    if j >= 2:
                        sum_probs(b, c, j - 2)
                weigh_values(b, c, J - 1, par, kind)
                sum_probs(b, c, J - 2)
                if after is not None:
                    scores(after[0], after[1], 0)
                    scores(after[0], after[1], 1)
                sum_probs(b, c, J - 1)
                if after is not None:
                    for u in range(2, 2 * J):
                        scores(after[0], after[1], u)

            pe.wait_ge(w_loaded, 7 * 16)
            pe.wait_ge(set_up, SETUPS)
            for t in range(KT):
                turn_ctx(0, "prologue", 0, t, 0)
            project_k(0, 0, "prologue", 0, 0, 0)
            project_k(0, 0, "prologue", 0, 1, 0)
            project_q(0, 0, "prologue", 0, 0, 0)
            for t in range(3):
                project_v(0, "prologue", 0, t, 0)
            for u in range(2 * J):
                scores(0, 0, u, prologue=True)
            steps(pe, chunk)
            for h in range(2):
                project_out(B - 1, h, "tail", 0, h, 1, 0)

        @block.scalar
        def _(act):
            def copy_ctx(b, kind, c, t, bk):
                i = wait_filled(act, bk, kind, c, ("ctx", t))
                act.activation(ctxT[:, :, t * KR:(t + 1) * KR],
                               proj_bank[i][:, 0:KC * KR].rearrange("p (k q) -> p k q", k=KC), ACT.Copy).then_inc(freed[i], 1)

            def high(b, cn, kind, c, bk):
                g = b * KC + cn
                for n, what in enumerate(("k0", "k1", "q")):
                    i = wait_filled(act, bk, kind, c, what)
                    if n == 0 and kind != "prologue":
                        for j in range(J):
                            act.wait_ge(stacked[j], g * 96)
                    if what == "q":
                        out, src, bias = q_hi[:], proj_bank[i][:, 0:N], bq_col
                    else:
                        out, src, bias = k_hi[:, n * HALF:(n + 1) * HALF], proj_bank[i][:, 0:HALF], bk_col
                    act.activation(out, src, ACT.Identity, bias=bias[:, cn:cn + 1]).then_inc(hi_ready, 1)

            def exps(b, c):
                g = b * KC + c
                for r in range(12):
                    j, a = divmod(r, 3)
                    act.wait_ge(st_in_psum, g * 12 + r + 1)
                    if a == 0 and j >= 2:
                        act.wait_ge(av_in_psum, g * 4 + j - 1)
                        act.wait_ge(sum_ready, g * 4 + j - 1)
                    if a == 0 and j < 2:
                        if not (isinstance(g, int) and g == 0):
                            act.wait_ge(av_in_psum, g * 4 + j - 1)
                            act.wait_ge(sum_ready, g * 4 + j - 1)
                    act.activation(probsT[j % 2][:, 2 * a:2 * a + 2, :].rearrange("k t q -> k (t q)"), ring[0:KR, r % 4, 0:2 * N],
                                   ACT.Exp, scale=SCALE).then_inc(exp_ready, 1)

            def chunk(b, c, kind, par, after):
                if c == 3 and kind != "last":
                    for t in range(KT):
                        copy_ctx(b + 1, kind, c, t, b)
                if after is not None:
                    high(after[0], after[1], kind, c, b)
                exps(b, c)

            act.wait_ge(w_loaded, 7 * 16)
            for t in range(KT):
                copy_ctx(0, "prologue", 0, t, 0)
            high(0, 0, "prologue", 0, 0)
            steps(act, chunk)

        @block.vector
        def _(dve):
            def low(b, cn, kind, c, bk):
                g = b * KC + cn
                for n, what in enumerate(("k0", "k1", "q")):
                    i, _ = uses.find(bk, kind, c, what)
                    dve.wait_ge(hi_ready, g * 3 + n + 1)
                    if what == "q":
                        out, src, bias, hi = q_lo[:], proj_bank[i][:, 0:N], bq_col, q_hi[:]
                    else:
                        out, src, bias, hi = (k_lo[:, n * HALF:(n + 1) * HALF], proj_bank[i][:, 0:HALF], bk_col,
                                              k_hi[:, n * HALF:(n + 1) * HALF])
                    dve.scalar_tensor_tensor(out=out, in0=src, scalar=bias[:, cn:cn + 1], in1=hi.bitcast(F32),
                                             op0=ALU.add, op1=ALU.subtract).then_inc(freed[i], 1)

            def negate(b, c):
                g = b * KC + c
                dve.wait_ge(max_ready, g * 8 + 8)
                dve.tensor_scalar(neg_max[:], row_max[c % 2][:], -1.0, None, ALU.mult).then_inc(neg_ready, 1)

            def copy_rows(b, kind, c):
                g = b * KC + c
                i = wait_filled(dve, b, kind, c, "m")
                if not (isinstance(g, int) and g == 0):
                    dve.wait_ge(max_placed, g * 16)
                dve.tensor_copy(neg_max_rows[:], proj_bank[i][0:2 * J, 0:QH]).then_inc(freed[i], 1)

            def values(b, kind, c, t, par, bk):
                i = wait_filled(dve, bk, kind, c, ("v", t))
                dve.tensor_tensor(v_tok[par][:, t, :], proj_bank[i][0:KR, :], bv_row[0:KR, :], ALU.add).then_inc(freed[i], 1)

            def add_out(b, h, kind, c, what, bk):
                i = wait_filled(dve, bk, kind, c, what)
                r = T["resid"][:, bass.ds(b * 2 + h, 1), :].rearrange("q a c -> q (a c)")
                dve.tensor_tensor(r, proj_bank[i][0:QH, :], r, ALU.add).then_inc(freed[i], 1)
                dve.wait_ge(freed[i], uses.find(bk, kind, c, what)[1])
                dve.memset(waited[:, 4:5], 0.0)
                dve.bn_stats(T["stats"][:, bass.ds(b * 2 + h, 1), :].rearrange("q a c -> q (a c)"), r)

            def make_mask(b, par):
                dve.wait_ge(mask_loaded, b * 16 + 16)
                dve.tensor_scalar(mask_bias[par][:, :, 0:NK], mask_int[:], 0.0, MASKED, ALU.is_equal, ALU.mult).then_inc(mask_ready, 1)

            def maxima(b, c, u, par):
                j, h = divmod(u, 2)
                pair = ring[0:QH, 2 * (u % 2):2 * (u % 2) + 2, 0:KH]
                dve.tensor_tensor_reduce(pair, pair,
                                         mask_bias[par][:, h, :].bitcast(F32).rearrange("q (a k) -> q a k", a=2), 1.0, -3.0e38,
                                         ALU.add, ALU.max, row_max[c % 2][:, u:u + 1]).then_inc(max_ready, 1)

            def wait_scores(b, c, u):
                dve.wait_ge(s_in_psum, (b * KC + c) * 8 + u + 1)
                dve.memset(waited[:, u % 4:u % 4 + 1], 0.0)

            def normalise(b, c, par):
                g = b * KC + c
                dve.wait_ge(den_in_psum, g * 4 + 4)
                dve.reciprocal(inv_den[:], av_bank[c % 2][:, 256:256 + N]).then_inc(inv_ready, 1)
                dve.wait_ge(inv_ready, g + 1)
                dve.tensor_tensor(attnT[par][:, c, :], av_bank[c % 2][:, 0:N], inv_den[:], ALU.mult).then_inc(attnT_ready, 1)

            def chunk(b, c, kind, par, after):
                negate(b, c)
                if after is not None:
                    low(after[0], after[1], kind, c, b)
                copy_rows(b, kind, c)
                if c == 0:
                    for t in range(3, KT):
                        values(b, kind, c, t, par, b)
                if c in (1, 2) and kind != "first":
                    add_out(b - 1, c - 1, kind, c, ("out", c - 1), b)
                if c == 3 and kind != "last":
                    for t in range(3):
                        values(b + 1, kind, c, t, 1 - par, b)
                if c == 2 and kind != "last":
                    make_mask(b + 1, 1 - par)
                if after is not None:
                    for u in range(2):
                        wait_scores(after[0], after[1], u)
                        maxima(after[0], after[1], u, after[2])
                normalise(b, c, par)
                if after is not None:
                    for u in range(2, 2 * J):
                        wait_scores(after[0], after[1], u)
                        maxima(after[0], after[1], u, after[2])

            for i in range(2):
                dve.memset(k_stack[i][R3:P].bitcast(F32), 1.0).then_inc(set_up, 1)
                dve.memset(k_stack[i][0:R3, :, NK:KP].bitcast(F32), 0.0).then_inc(set_up, 1)
                dve.memset(q_stack[i][R3:P].bitcast(F32), 0.0).then_inc(set_up, 1)
                dve.memset(mask_bias[i][:, :, NK:KP].bitcast(F32), MASKED).then_inc(set_up, 1)
            dve.memset(ones[:], 1.0).then_inc(set_up, 1)
            dve.tensor_copy(ident_r[:], T["ident"][:]).then_inc(set_up, 1)
            make_mask(0, 0)
            dve.wait_ge(w_loaded, 7 * 16)
            low(0, 0, "prologue", 0, 0)
            for t in range(3):
                values(0, "prologue", 0, t, 0, 0)
            for u in range(2 * J):
                wait_scores(0, 0, u)
                maxima(0, 0, u, 0)
            steps(dve, chunk)
            for h in range(2):
                add_out(B - 1, h, "tail", 0, h, 0)

        @block.gpsimd
        def _(pool):
            def chunk(b, c, kind, par, after):
                g = b * KC + c
                for j in range(J):
                    n = g * J + j
                    if not (isinstance(n, int) and n == 0):
                        pool.wait_ge(sum_ready, n)
                    pool.wait_ge(exp_ready, g * 12 + 3 * j + 3)
                    pool.tensor_tensor(half_sum[:], probsT[j % 2][:, 0:3, :], probsT[j % 2][:, 3:6, :], ALU.add).then_inc(halves_added, 1)
                    pool.wait_ge(halves_added, n * 2 + 1)
                    pool.tensor_tensor(half_sum[:, 0, :], half_sum[:, 0, :], half_sum[:, 1, :], ALU.add).then_inc(halves_added, 1)
                    if not (isinstance(n, int) and n < 2):
                        pool.wait_ge(den_in_psum, n - 1)
                    pool.wait_ge(halves_added, n * 2 + 2)
                    pool.tensor_tensor(key_sum[j % 2][:], half_sum[:, 0, :], half_sum[:, 2, :], ALU.add).then_inc(sum_ready, 1)
            steps(pool, chunk)


SETUPS = 10


def route(nc, S, T):
    B, N, C, QH, E = S["B"], S["N"], S["C"], S["QH"], S["E"]
    ROWS, TILES = 2 * B, S["TILES"]
    STEPS = -(-B * N // P)
    with ExitStack() as ctx:
        def sb(n, shape, dt=F32):
            return ctx.enter_context(nc.sbuf_tensor(f"r_{n}", shape, dt))

        def sem(n):
            return ctx.enter_context(nc.semaphore(f"r_{n}"))

        rank_bank = ctx.enter_context(nc.psum_tensor("r_rank", [P, ROWS, E], F32))
        total_bank = ctx.enter_context(nc.psum_tensor("r_total", [P, 512], F32))
        before = sb("before", [QH, QH])
        ones = sb("ones", [QH, QH])
        order = sb("order", [QH, E])
        thresholds = sb("thresholds", [QH, STEPS])
        earlier = sb("earlier", [QH, E, E])
        tile_no = sb("tile_no", [QH, TILES])
        prob = sb("prob", [QH, ROWS, E])
        rest = sb("rest", [QH, ROWS, E])
        work = sb("work", [QH, ROWS, E])
        pick = [sb(f"pick{i}", [QH, ROWS, E]) for i in range(2)]
        both = sb("both", [QH, ROWS, E])
        best = [sb(f"best{i}", [QH, ROWS]) for i in range(2)]
        col = sb("col", [QH, ROWS])
        col2 = sb("col2", [QH, ROWS])
        count = sb("count", [QH, E])
        over = sb("over", [QH, E, STEPS])
        tiles = sb("tiles", [QH, E])
        share = sb("share", [QH, E, E])
        first_tile = sb("first_tile", [QH, E])
        slot_f = sb("slot_f", [QH, ROWS])
        passed = sb("passed", [QH, TILES, E])
        expert_f = sb("expert_f", [QH, TILES])

        made = sem("made")
        step = sem("step")
        logits_less_max = sem("logits_less_max")
        exp_ready = sem("exp_ready")
        picks_ready = sem("picks_ready")
        ranks_ready = sem("ranks_ready")
        slots_ready = sem("slots_ready")
        scattered = sem("scattered")
        stored = sem("stored")
        block = ctx.enter_context(nc.Block())

        def per_row(a):
            return a.rearrange("q (r a) -> q r a", a=1).broadcast_to([QH, ROWS, E])

        def per_expert(a):
            return a.rearrange("q (a e) -> q a e", a=1).broadcast_to([QH, ROWS, E])

        @block.gpsimd
        def _(pool):
            pool.memset(before[:], 1.0).then_inc(made, 1)
            pool.memset(ones[:], 1.0).then_inc(made, 1)
            pool.memset(earlier[:], 1.0).then_inc(made, 1)
            pool.iota(order[:], pattern=[[-1, E]], base=E, channel_multiplier=0, allow_small_or_imprecise_dtypes=True).then_inc(made, 1)
            pool.iota(thresholds[:], pattern=[[P, STEPS]], base=0, channel_multiplier=0, allow_small_or_imprecise_dtypes=True).then_inc(made, 1)
            pool.iota(tile_no[:], pattern=[[1, TILES]], base=0, channel_multiplier=0, allow_small_or_imprecise_dtypes=True).then_inc(made, 1)
            pool.wait_ge(made, 6)
            pool.affine_select(out=before[:], in_=before[:], compare_op=ALU.is_gt, fill=0.0, base=0,
                               pattern=[[1, QH]], channel_multiplier=-1).then_inc(made, 1)
            pool.affine_select(out=earlier[:], in_=earlier[:], compare_op=ALU.is_gt, fill=0.0, base=0,
                               pattern=[[1, E], [-1, E]], channel_multiplier=0).then_inc(made, 1)
            pool.wait_ge(slots_ready, 1)
            for r in range(ROWS):
                for i in range(2):
                    pool.indirect_dma_start(out=S["x_rows"], out_offset=bass.IndirectOffsetOnAxis(ap=T["slot"][:, i, r:r + 1], axis=0),
                                            in_=T["resid"][:, r, :], in_offset=None).then_inc(scattered, 16)
            pool.wait_ge(scattered, 2 * ROWS * 16)

        @block.scalar
        def _(act):
            act.wait_ge(logits_less_max, 1)
            act.activation(prob[:], work[:], ACT.Exp).then_inc(exp_ready, 1)

        @block.tensor
        def _(pe):
            pe.wait_ge(made, 8)
            pe.wait_ge(picks_ready, 1)
            pe.matmul(rank_bank[0:QH].rearrange("q r e -> q (r e)"), before[:], both[:].rearrange("q r e -> q (r e)"),
                      start=True, stop=True, skip_group_check=True)
            for r in range(ROWS - 1):
                pe.matmul(rank_bank[0:QH, r + 1:ROWS, :], ones[:],
                          both[:, r:r + 1, :].broadcast_to([QH, ROWS - 1 - r, E]), start=False, stop=True,
                          skip_group_check=True)
            for r in range(ROWS):
                mm = pe.matmul(total_bank[0:QH, 0:E], ones[:], both[:, r, :], start=(r == 0), stop=(r == ROWS - 1))
            mm.then_inc(ranks_ready, 1)

        @block.vector
        def _(dve):
            done = [0]

            def then(ins):
                done[0] += 1
                ins.then_inc(step, 1)
                dve.wait_ge(step, done[0])

            def choose(source, i):
                then(dve.tensor_reduce(best[i][:], source, AX_X, ALU.max))
                then(dve.tensor_tensor(work[:], source, per_row(best[i][:]), ALU.is_equal))
                then(dve.tensor_tensor(work[:], work[:], per_expert(order[:]), ALU.mult))
                then(dve.tensor_reduce(col[:], work[:], AX_X, ALU.max))
                then(dve.tensor_tensor(pick[i][:], work[:], per_row(col[:]), ALU.is_equal))

            dve.wait_ge(made, 8)
            then(dve.tensor_reduce(col[:], T["logits"][:], AX_X, ALU.max))
            dve.tensor_tensor(work[:], T["logits"][:], per_row(col[:]), ALU.subtract).then_inc(logits_less_max, 1)
            dve.wait_ge(exp_ready, 1)
            then(dve.tensor_reduce(col[:], prob[:], AX_X, ALU.add))
            then(dve.reciprocal(col2[:], col[:]))
            then(dve.tensor_tensor(prob[:], prob[:], per_row(col2[:]), ALU.mult))
            choose(prob[:], 0)
            then(dve.scalar_tensor_tensor(out=rest[:].rearrange("q r e -> q (r e)"), in0=pick[0][:].rearrange("q r e -> q (r e)"),
                                          scalar=-4.0, in1=prob[:].rearrange("q r e -> q (r e)"), op0=ALU.mult, op1=ALU.add))
            choose(rest[:], 1)
            dve.tensor_tensor(both[:], pick[0][:], pick[1][:], ALU.add).then_inc(picks_ready, 1)
            then(dve.tensor_tensor(col[:], best[0][:], best[1][:], ALU.add))
            then(dve.reciprocal(col2[:], col[:]))
            for i in range(2):
                then(dve.tensor_tensor(T["share"][:, i, :], best[i][:], col2[:], ALU.mult))
            dve.wait_ge(ranks_ready, 1)
            then(dve.tensor_copy(count[:], total_bank[0:QH, 0:E]))
            then(dve.tensor_tensor(over[:], count[:].rearrange("q (e a) -> q e a", a=1).broadcast_to([QH, E, STEPS]),
                                   thresholds[:].rearrange("q (a s) -> q a s", a=1).broadcast_to([QH, E, STEPS]), ALU.is_gt))
            then(dve.tensor_reduce(tiles[:], over[:], AX_X, ALU.add))
            then(dve.tensor_tensor(share[:], earlier[:], tiles[:].rearrange("q (a e) -> q a e", a=1).broadcast_to([QH, E, E]), ALU.mult))
            then(dve.tensor_reduce(first_tile[:], share[:], AX_X, ALU.add))
            then(dve.tensor_scalar(count[:], first_tile[:], float(P), None, ALU.mult))
            then(dve.tensor_tensor(rest[:], rank_bank[0:QH], per_expert(count[:]), ALU.add))
            for i in range(2):
                then(dve.tensor_tensor(work[:], pick[i][:], rest[:], ALU.mult))
                then(dve.tensor_reduce(slot_f[:], work[:], AX_X, ALU.add))
                then(dve.tensor_copy(T["slot"][:, i, :], slot_f[:]))
            then(dve.tensor_tensor(passed[:], tile_no[:].rearrange("q (t a) -> q t a", a=1).broadcast_to([QH, TILES, E]),
                                   first_tile[:].rearrange("q (a e) -> q a e", a=1).broadcast_to([QH, TILES, E]), ALU.is_ge))
            then(dve.tensor_reduce(expert_f[:], passed[:, :, 1:E], AX_X, ALU.add))
            then(dve.tensor_copy(T["expert"][:, 0:TILES], expert_f[0:1, :]))
            dve.memset(col[:], 0.0).then_inc(slots_ready, 1)


def experts(nc, S, T):
    C, E, F, TILES = S["C"], S["E"], S["F"], S["TILES"]
    KC, FC = C // P, F // P
    GU = 2 * F // 512
    with ExitStack() as ctx:
        def sb(n, shape, dt=F32):
            return ctx.enter_context(nc.sbuf_tensor(f"e_{n}", shape, dt))

        def sem(n):
            return ctx.enter_context(nc.semaphore(f"e_{n}"))

        gate_bank = ctx.enter_context(nc.psum_tensor("e_gate", [P, 2, 512], F32))
        up_bank = ctx.enter_context(nc.psum_tensor("e_up", [P, 2, 512], F32))
        h_bank = [ctx.enter_context(nc.psum_tensor(f"e_h{i}", [P, 512], F32)) for i in range(2)]
        x_bank = ctx.enter_context(nc.psum_tensor("e_x", [P, 512], F32))
        y_bank = ctx.enter_context(nc.psum_tensor("e_y", [P, 512], F32))

        w_gu = [sb(f"w_gu{i}", [P, KC, 2 * F]) for i in range(2)]
        w_down = [sb(f"w_down{i}", [P, FC, C]) for i in range(2)]
        x_rows = [sb(f"x_rows{i}", [P, C]) for i in range(2)]
        xT = [sb(f"xT{i}", [P, KC, P]) for i in range(2)]
        gate = [sb(f"gate{i}", [P, F]) for i in range(2)]
        hidden = [sb(f"hidden{i}", [P, F]) for i in range(2)]
        hiddenT = sb("hiddenT", [P, FC, P])
        y_rows = [sb(f"y_rows{i}", [P, C]) for i in range(2)]

        w_gu_loaded = [sem(f"w_gu_loaded{i}") for i in range(2)]
        w_down_loaded = [sem(f"w_down_loaded{i}") for i in range(2)]
        x_loaded = [sem(f"x_loaded{i}") for i in range(2)]
        xT_in_psum = sem("xT_in_psum")
        xT_ready = sem("xT_ready")
        gu_in_psum = sem("gu_in_psum")
        silu_ready = sem("silu_ready")
        hidden_ready = sem("hidden_ready")
        hT_in_psum = sem("hT_in_psum")
        hT_ready = sem("hT_ready")
        y_in_psum = sem("y_in_psum")
        y_ready = sem("y_ready")
        y_stored = [sem(f"y_stored{i}") for i in range(2)]
        block = ctx.enter_context(nc.Block())

        def steps(eng, tile):
            tile(0, 0, 0)
            tile(1, 1, 0)
            tile(2, 0, 1)
            with eng.Fori(1, (TILES - 3) // 2) as pair:
                tile(pair * 2 + 1, 1, pair)
                tile(pair * 2 + 2, 0, pair + 1)
            tile(TILES - 2, 1, (TILES - 2) // 2)
            tile(TILES - 1, 0, (TILES - 1) // 2)

        @block.sync
        def _(sp):
            def load(t, par):
                e = sp.value_load(T["expert"][0:1, bass.ds(t, 1)], min_val=0, max_val=E - 1)
                sp.dma_start(x_rows[par][:], S["x_rows"].rearrange("(t p) c -> t p c", p=P)[bass.ds(t, 1)].rearrange("a p c -> (a p) c")).then_inc(x_loaded[par], 16)
                sp.dma_start(w_gu[par][:], S["gate_up_w"].rearrange("e (k p) n -> e p k n", p=P)[bass.ds(e, 1)].rearrange("a p k n -> (a p) k n")).then_inc(w_gu_loaded[par], 16)
                return e

            def load_down(e, par):
                sp.dma_start(w_down[par][:], S["down_w"].rearrange("e (k p) n -> e p k n", p=P)[bass.ds(e, 1)].rearrange("a p k n -> (a p) k n")).then_inc(w_down_loaded[par], 16)

            def tile(t, par, turn):
                if not (isinstance(t, int) and t + 2 >= TILES):
                    sp.wait_ge(gu_in_psum, t * 2 + 2)
                    e = load(t + 2, par)
                    sp.wait_ge(y_in_psum, t + 1)
                    load_down(e, par)

            for t in range(2):
                load_down(load(t, t), t)
            steps(sp, tile)

        @block.scalar
        def _(act):
            def tile(t, par, turn):
                for a in range(2):
                    act.wait_ge(gu_in_psum, t * 2 + a + 1)
                    act.activation(gate[par][:, a * 512:(a + 1) * 512], gate_bank[:, a, :], ACT.Silu).then_inc(silu_ready, 1)
                if not (isinstance(t, int) and t == 0):
                    finish(t - 1, 1 - par, turn if par == 1 else turn - 1)
                if isinstance(t, int) and t == TILES - 1:
                    finish(t, par, turn)

            def finish(t, par, turn):
                for a in range(2):
                    act.wait_ge(hT_in_psum, t * 2 + a + 1)
                    act.activation(hiddenT[:, 4 * a:4 * a + 4, :].rearrange("p k q -> p (k q)"), h_bank[a][:], ACT.Copy).then_inc(hT_ready, 1)
                act.wait_ge(y_in_psum, t + 1)
                if not (isinstance(turn, int) and turn == 0):
                    act.wait_ge(y_stored[par], turn * 16)
                act.activation(y_rows[par][:], y_bank[:], ACT.Copy).then_inc(y_ready, 1)

            steps(act, tile)

        @block.vector
        def _(dve):
            def copy_xT(t, par):
                dve.wait_ge(xT_in_psum, t + 1)
                dve.tensor_copy(xT[par][:].rearrange("p k q -> p (k q)"), x_bank[:]).then_inc(xT_ready, 1)

            def tile(t, par, turn):
                if not (isinstance(t, int) and t == TILES - 1):
                    copy_xT(t + 1, 1 - par)
                for a in range(2):
                    dve.wait_ge(silu_ready, t * 2 + a + 1)
                    dve.tensor_tensor(hidden[par][:, a * 512:(a + 1) * 512], up_bank[:, a, :], gate[par][:, a * 512:(a + 1) * 512],
                                      ALU.mult).then_inc(hidden_ready, 1)
            copy_xT(0, 0)
            steps(dve, tile)

        @block.gpsimd
        def _(pool):
            def tile(t, par, turn):
                pool.wait_ge(y_ready, t + 1)
                pool.dma_start(S["y_rows"].rearrange("(t p) c -> t p c", p=P)[bass.ds(t, 1)].rearrange("a p c -> (a p) c"), y_rows[par][:]).then_inc(y_stored[par], 16)
            steps(pool, tile)
            for i in range(2):
                pool.wait_ge(y_stored[i], (TILES - i + 1) // 2 * 16)

        @block.tensor
        def _(pe):
            def turn_x(t, par, turn):
                pe.wait_ge(x_loaded[par], turn * 16 + 16)
                if not (isinstance(t, int) and t == 0):
                    pe.wait_ge(xT_ready, t)
                for k in range(KC):
                    mm = pe.transpose(x_bank[:, k * P:(k + 1) * P], x_rows[par][:, k * P:(k + 1) * P], T["ident"][:])
                mm.then_inc(xT_in_psum, 1)

            def gate_up(t, par, turn):
                pe.wait_ge(xT_ready, t + 1)
                pe.wait_ge(w_gu_loaded[par], turn * 16 + 16)
                for a in range(2):
                    if not (isinstance(t, int) and t == 0):
                        pe.wait_ge(hidden_ready, t * 2 - 1 + a)
                    for bank, first in ((gate_bank, 0), (up_bank, F)):
                        for k in range(KC):
                            mm = pe.matmul(bank[:, a, :], xT[par][:, k, :], w_gu[par][:, k, first + a * 512:first + (a + 1) * 512],
                                           start=(k == 0), stop=(k == KC - 1))
                    mm.then_inc(gu_in_psum, 1)

            def down(t, par, turn):
                for a in range(2):
                    pe.wait_ge(hidden_ready, t * 2 + a + 1)
                    for k in range(4):
                        f = 4 * a + k
                        mm = pe.transpose(h_bank[a][:, k * P:(k + 1) * P], hidden[par][:, f * P:(f + 1) * P], T["ident"][:])
                    mm.then_inc(hT_in_psum, 1)
                pe.wait_ge(w_down_loaded[par], turn * 16 + 16)
                if not (isinstance(t, int) and t == 0):
                    pe.wait_ge(y_ready, t)
                for f in range(FC):
                    if f % 4 == 0:
                        pe.wait_ge(hT_ready, t * 2 + f // 4 + 1)
                    mm = pe.matmul(y_bank[:], hiddenT[:, f, :], w_down[par][:, f, :], start=(f == 0), stop=(f == FC - 1))
                mm.then_inc(y_in_psum, 1)

            def tile(t, par, turn):
                if not (isinstance(t, int) and t == TILES - 1):
                    turn_x(t + 1, 1 - par, turn if par == 0 else turn + 1)
                gate_up(t, par, turn)
                if not (isinstance(t, int) and t == 0):
                    down(t - 1, 1 - par, turn if par == 1 else turn - 1)
                if isinstance(t, int) and t == TILES - 1:
                    down(t, par, turn)
            turn_x(0, 0, 0)
            steps(pe, tile)


def combine(nc, S, T):
    B, N, C, QH = S["B"], S["N"], S["C"], S["QH"]
    ROWS = 2 * B
    RING = 4
    with ExitStack() as ctx:
        def sb(n, shape, dt=F32):
            return ctx.enter_context(nc.sbuf_tensor(f"f_{n}", shape, dt))

        def sem(n):
            return ctx.enter_context(nc.semaphore(f"f_{n}"))
        y = [sb(f"y{i}", [QH, 2, C]) for i in range(RING)]
        std, rstd, eps = sb("std", [QH, ROWS]), sb("rstd", [QH, ROWS]), sb("eps", [QH, 1])
        gathered = [sem(f"gathered{i}") for i in range(RING)]
        added = sem("added")
        stats_ready = sem("stats_ready")
        var_ready = sem("var_ready")
        std_ready = sem("std_ready")
        rstd_ready = sem("rstd_ready")
        normed = sem("normed")
        stored = sem("stored")
        block = ctx.enter_context(nc.Block())

        @block.gpsimd
        def _(pool):
            for r in range(ROWS):
                if r >= RING:
                    pool.wait_ge(added, 2 * (r - RING) + 2)
                for i in range(2):
                    pool.indirect_dma_start(out=y[r % RING][:, i, :], out_offset=None, in_=S["y_rows"],
                                            in_offset=bass.IndirectOffsetOnAxis(ap=T["slot"][:, i, r:r + 1], axis=0)).then_inc(gathered[r % RING], 16)

        @block.vector
        def _(dve):
            dve.memset(eps[:], LN_EPS).then_inc(var_ready, 1)
            for r in range(ROWS):
                dve.wait_ge(gathered[r % RING], 32 * (r // RING + 1))
                for i in range(2):
                    dve.scalar_tensor_tensor(out=T["resid"][:, r, :], in0=y[r % RING][:, i, :], scalar=T["share"][:, i, r:r + 1],
                                             in1=T["resid"][:, r, :], op0=ALU.mult, op1=ALU.add).then_inc(added, 1)
                    dve.wait_ge(added, 2 * r + i + 1)
                dve.bn_stats(T["stats"][:, r, :], T["resid"][:, r, :]).then_inc(stats_ready, 1)
                dve.wait_ge(stats_ready, r + 1)
                dve.bn_aggr(T["mean_var"][:, r, :], T["stats"][:, r, :]).then_inc(var_ready, 1)
            dve.wait_ge(std_ready, 1)
            dve.reciprocal(rstd[:], std[:]).then_inc(rstd_ready, 1)
            dve.wait_ge(rstd_ready, 1)
            for r in range(ROWS):
                dve.tensor_scalar(T["resid"][:, r, :], T["resid"][:, r, :], T["mean_var"][:, r, 0:1], rstd[:, r:r + 1],
                                  ALU.subtract, ALU.mult).then_inc(normed, 1)

        @block.scalar
        def _(act):
            act.wait_ge(var_ready, ROWS + 1)
            act.activation(std[:], T["mean_var"][:, :, 1], ACT.Sqrt, bias=eps[:]).then_inc(std_ready, 1)

        @block.sync
        def _(sp):
            rows = S["out"].rearrange("b (h q) c -> (b h) q c", q=QH)
            for r in range(0, ROWS, 4):
                sp.wait_ge(normed, r + 4)
                sp.dma_start(rows[r:r + 4].rearrange("r q c -> q r c"), T["resid"][:, r:r + 4, :]).then_inc(stored, 16)
            sp.wait_ge(stored, ROWS // 4 * 16)


def build(nc, x, ctx_in, mask, Wqkv, Wproj, bproj, Wq, bq, Wk, bk, Wv, bv, Wo, bo, gate_w, gate_up_w, down_w, out):
    B, N, C = x.shape
    S = dict(x=x, ctx=ctx_in, mask=mask, Wqkv=Wqkv, Wproj=Wproj, bproj=bproj, Wq=Wq, bq=bq, Wk=Wk, bk=bk, Wv=Wv, bv=bv,
             Wo=Wo, bo=bo, gate_w=gate_w, gate_up_w=gate_up_w, down_w=down_w, out=out, B=B, N=N, C=C)
    S["H"] = 16
    S["HD"] = C // S["H"]
    S["W"] = 8
    S["QH"] = N // 2
    S["KW"] = S["QH"] + S["W"]
    S["KEY0"] = N - S["KW"]
    S["E"], S["F"] = down_w.shape[0:2]
    S["TILES"] = 2 * B * N // P + S["E"] - 1
    S["xT"] = nc.dram_tensor("xT_scratch", (2 * B, P, C // P, S["QH"]), F32, kind="Internal").ap()
    S["x_rows"] = nc.dram_tensor("x_rows_scratch", (S["TILES"] * P, C), F32, kind="Internal").ap()
    S["y_rows"] = nc.dram_tensor("y_rows_scratch", (S["TILES"] * P, C), F32, kind="Internal").ap()
    with ExitStack() as ctx:
        def sb(name, shape, dt=F32):
            return ctx.enter_context(nc.sbuf_tensor(name, shape, dt))
        QH, ROWS = S["QH"], 2 * B
        T = dict(ident=sb("ident", [P, P]), resid=sb("resid", [QH, ROWS, C]), stats=sb("stats", [QH, ROWS, 6]),
                 mean_var=sb("mean_var", [QH, ROWS, 2]), logits=sb("logits", [QH, ROWS, S["E"]]),
                 slot=sb("slot", [QH, 2, ROWS], U32), share=sb("top_share", [QH, 2, ROWS]), expert=sb("expert", [1, S["TILES"] + 1], I32))
        with ExitStack() as actx:
            T["bias_row"] = actx.enter_context(nc.sbuf_tensor("bias_row", [QH, C], F32))
            T["zeros"] = actx.enter_context(nc.sbuf_tensor("zeros", [P, C], F32))
            T["band"] = actx.enter_context(nc.sbuf_tensor("band", [QH, 2, S["KW"]], F32))
            T["wqkv"] = actx.enter_context(nc.sbuf_tensor("wqkv", [P, C // P, 3 * C], F32))
            T["wproj"] = actx.enter_context(nc.sbuf_tensor("wproj", [P, C // P, C], F32))
            make_constants(nc, S, T)
            self_attention(nc, S, T)
        with ExitStack() as bctx:
            T["bias_row"] = bctx.enter_context(nc.sbuf_tensor("bias_row2", [QH, C], F32))
            normalise_and_turn(nc, S, T, "n1", bias=S["bo"])
        cross_attention(nc, S, T)
        normalise_and_turn(nc, S, T, "n2", router=True)
        route(nc, S, T)
        experts(nc, S, T)
        combine(nc, S, T)


_INS = ["x", "ctx_1024", "mask_BxSxS2_ik1", "L0_attn_Wqkv", "L0_attn_Wproj", "L0_attn_bproj", "L0_xattn_Wq", "L0_xattn_bq",
        "L0_xattn_Wk", "L0_xattn_bk", "L0_xattn_Wv", "L0_xattn_bv", "L0_xattn_Wo", "L0_xattn_bo", "L0_ffn_gate_w",
        "L0_ffn_gate_up_w", "L0_ffn_down_w"]


def kernel(**inputs):
    import numpy as _np
    import concourse.bacc as _bacc
    from concourse import mybir as _mybir
    from concourse.bass_utils import run_bass_kernel_spmd as _run

    nc = _bacc.Bacc("TRN2", target_bir_lowering=False, num_devices=1)
    arrays, args = {}, []
    for name in _INS:
        a = _np.ascontiguousarray(inputs[name])
        arrays[f"in_{name}_dram"] = a
        args.append(nc.dram_tensor(f"in_{name}_dram", a.shape, _mybir.dt.from_np(a.dtype), kind="ExternalInput").ap())
    args.append(nc.dram_tensor("out_dram", inputs["x"].shape, _mybir.dt.float32, kind="ExternalOutput").ap())
    build(nc, *args)
    r = _run(nc, [arrays], core_ids=[0])
    return r.results[0]["out_dram"]
```

```python
from contextlib import ExitStack

import concourse.bass as bass
from concourse import mybir

ALU = mybir.AluOpType
ACT = mybir.ActivationFunctionType
AX_X = mybir.AxisListType.X
F32 = mybir.dt.float32
F32R = mybir.dt.float32r
I32 = mybir.dt.int32
U32 = mybir.dt.uint32

P = 128
MASKED = -float(2 ** 100)
LN_EPS = 1e-5


def make_constants(nc, S, T):
    B, N, C, QH = S["B"], S["N"], S["C"], S["QH"]
    with ExitStack() as ctx:
        zeroed = ctx.enter_context(nc.semaphore("zeroed"))
        made = ctx.enter_context(nc.semaphore("made"))
        rows_zeroed = ctx.enter_context(nc.semaphore("rows_zeroed"))
        loaded = ctx.enter_context(nc.semaphore("const_loaded"))
        block = ctx.enter_context(nc.Block())

        @block.sync
        def _(sp):
            sp.dma_start(T["wqkv"][:], S["Wqkv"].rearrange("(k p) n -> p k n", p=P)).then_inc(loaded, 16)
            sp.dma_start(T["wproj"][:], S["Wproj"].rearrange("(k p) n -> p k n", p=P)).then_inc(loaded, 16)
            sp.dma_start(T["resid"][:], S["x"].rearrange("b (h q) c -> q (b h) c", q=QH)).then_inc(loaded, 16)
            sp.dma_start(T["bias_row"][:], S["bproj"].rearrange("(a n) -> a n", a=1).broadcast_to([QH, C])).then_inc(loaded, 16)
            sp.wait_ge(zeroed, 3)
            sp.dma_start(S["x_rows"].rearrange("(t p) c -> p t c", p=P),
                         T["zeros"][:].rearrange("p (a c) -> p a c", a=1).broadcast_to([P, S["TILES"], C])).then_inc(rows_zeroed, 16)
            sp.wait_ge(loaded, 4 * 16)
            sp.wait_ge(rows_zeroed, 16)

        @block.gpsimd
        def _(pool):
            pool.memset(T["ident"][:], 0.0).then_inc(zeroed, 1)
            pool.memset(T["band"][:], 0.0).then_inc(zeroed, 1)
            pool.memset(T["zeros"][:], 0.0).then_inc(zeroed, 1)
            pool.wait_ge(zeroed, 3)
            pool.affine_select(out=T["ident"][:], in_=T["ident"][:], compare_op=ALU.not_equal, fill=1.0,
                               base=0, pattern=[[-1, P]], channel_multiplier=1).then_inc(made, 1)
            for h in range(2):
                off = h * (QH - S["KEY0"])
                b = T["band"][:, h, :]
                pool.affine_select(out=b, in_=b, compare_op=ALU.is_ge, fill=MASKED, base=S["W"] - off,
                                   pattern=[[1, S["KW"]]], channel_multiplier=-1).then_inc(made, 1)
                pool.wait_ge(made, 2 * h + 2)
                pool.affine_select(out=b, in_=b, compare_op=ALU.is_ge, fill=MASKED, base=S["W"] + off,
                                   pattern=[[-1, S["KW"]]], channel_multiplier=1).then_inc(made, 1)
            pool.wait_ge(made, 5)


def self_attention(nc, S, T):
    B, N, C, H, HD, QH, KW, KEY0 = (S[k] for k in ("B", "N", "C", "H", "HD", "QH", "KW", "KEY0"))
    KC = C // P
    J = P // HD
    UNITS = 2 * KC
    SCALE = HD ** -0.5
    with ExitStack() as ctx:
        def sb(name, shape, dt=F32):
            return ctx.enter_context(nc.sbuf_tensor(name, shape, dt))

        def sem(name):
            return ctx.enter_context(nc.semaphore(name))

        bank = [ctx.enter_context(nc.psum_tensor(f"a_bank{i}", [P, 512], F32)) for i in range(8)]
        score_bank, pt_bank, av_bank, proj_bank = bank[0:2], bank[2:4], bank[4:6], bank[6:8]

        x_tok = sb("a_x_tok", [QH, 2, C])
        xT = sb("a_xT", [P, KC, N])
        qk_hi = sb("a_qk_hi", [P, 2 * KC, N], F32R)
        qk_lo = sb("a_qk_lo", [P, 2 * KC, N], F32R)
        q_stack = sb("a_q_stack", [P, J, KC, N], F32R)
        k_stack = sb("a_k_stack", [P, J, KC, N], F32R)
        v_tok = [sb(f"a_v_tok{i}", [KW, 2, C]) for i in range(2)]
        probs = sb("a_probs", [QH, UNITS, J, KW])
        row_max = sb("a_row_max", [QH, UNITS, J])
        neg_max = sb("a_neg_max", [QH, UNITS, J])
        row_sum = sb("a_row_sum", [QH, UNITS, J])
        inv_sum = sb("a_inv_sum", [QH, UNITS, J])
        probsT = [sb(f"a_probsT{i}", [KW, J, QH]) for i in range(2)]
        attnT = [sb(f"a_attnT{i}", [P, KC, QH]) for i in range(2)]
        waited = sb("a_waited", [QH, 1])

        x_loaded = sem("x_loaded")
        xT_in_psum = sem("xT_in_psum")
        xT_ready = sem("xT_ready")
        qk_in_psum = sem("qk_in_psum")
        qk_hi_ready = sem("qk_hi_ready")
        qk_lo_ready = sem("qk_lo_ready")
        v_in_psum = sem("v_in_psum")
        v_ready = sem("v_ready")
        q_stacked = sem("q_stacked")
        k_stacked = sem("k_stacked")
        scores_in_psum = sem("scores_in_psum")
        masked_ready = sem("masked_ready")
        max_ready = sem("max_ready")
        exp_ready = sem("exp_ready")
        inv_ready = sem("inv_ready")
        probs_ready = sem("probs_ready")
        pT_in_psum = sem("pT_in_psum")
        pT_ready = sem("pT_ready")
        av_in_psum = sem("av_in_psum")
        attnT_ready = sem("attnT_ready")
        out_in_psum = sem("out_in_psum")
        out_added = sem("out_added")
        bias_added = sem("bias_added")

        block = ctx.enter_context(nc.Block())

        def steps(eng, step):
            with eng.Fori(0, B // 2 - 1) as pair:
                step(pair * 2, 0)
                step(pair * 2 + 1, 1)
            step(B - 2, 0)
            step(B - 1, 1, last=True)

        @block.sync
        def _(sp):
            def load_x(b):
                sp.dma_start(x_tok[:], S["x"].rearrange("b (h q) c -> b q h c", q=QH)[bass.ds(b, 1)].rearrange("a q h c -> (a q) h c")).then_inc(x_loaded, 16)

            def stack(b):
                sp.wait_ge(qk_hi_ready, b * 8 + 8)
                sp.wait_ge(qk_lo_ready, b * 8 + 8)
                for dst, first, order, done in ((q_stack, 0, (qk_hi, qk_hi, qk_lo, qk_lo), q_stacked),
                                                (k_stack, KC, (qk_hi, qk_lo, qk_hi, qk_lo), k_stacked)):
                    for g, src in enumerate(order):
                        for j in range(J):
                            sp.dma_start(dst[HD * g:HD * g + HD, j].bitcast(F32), src[HD * j:HD * j + HD, first:first + KC].bitcast(F32)).then_inc(done, 16)

            def step(b, par, last=False):
                if last:
                    return
                sp.wait_ge(scores_in_psum, b * 8 + 8)
                stack(b + 1)
                if not (isinstance(b, int) and b == B - 2):
                    load_x(b + 2)
            load_x(0)
            sp.wait_ge(xT_in_psum, 2)
            stack(0)
            load_x(1)
            steps(sp, step)

        @block.tensor
        def _(pe):
            def transposes(b, par):
                pe.wait_ge(x_loaded, b * 16 + 16)
                for h in range(2):
                    if not (isinstance(b, int) and b == 0):
                        pe.wait_ge(v_ready, b * 2 - 1 + h)
                        pe.wait_ge(out_added, b * 2 - 1 + h)
                    for k in range(KC):
                        last = pe.transpose(proj_bank[h][:, k * QH:(k + 1) * QH], x_tok[:, h, k * P:(k + 1) * P],
                                            T["ident"][0:QH, 0:QH])
                    last.then_inc(xT_in_psum, 1)

            def project_qk(b, n):
                if n < 2:
                    pe.wait_ge(xT_ready, b * 2 + 2)
                else:
                    pe.wait_ge(qk_lo_ready, b * 8 + n - 1)
                for k in range(KC):
                    last = pe.matmul(proj_bank[n % 2][:, 0:N], T["wqkv"][:, k, n * P:(n + 1) * P], xT[:, k, :],
                                     start=(k == 0), stop=(k == KC - 1))
                last.then_inc(qk_in_psum, 1)

            def project_v(b, w):
                pe.wait_ge(qk_lo_ready, b * 8 + 7 + w)
                for k in range(KC):
                    last = pe.matmul(proj_bank[w][0:KW, :], xT[:, k, KEY0 * w:KEY0 * w + KW], T["wqkv"][:, k, 2 * C:3 * C],
                                     start=(k == 0), stop=(k == KC - 1))
                last.then_inc(v_in_psum, 1)

            def scores(b, u):
                h, c = divmod(u, KC)
                if u == 0:
                    pe.wait_ge(q_stacked, b * 256 + 256)
                    pe.wait_ge(k_stacked, b * 256 + 256)
                if u >= 2:
                    pe.wait_ge(masked_ready, b * 8 + u - 1)
                for j in range(J):
                    last = pe.matmul(score_bank[u % 2][0:QH, j * KW:(j + 1) * KW], q_stack[:, j, c, h * QH:(h + 1) * QH],
                                     k_stack[:, j, c, KEY0 * h:KEY0 * h + KW], start=True, stop=True)
                last.then_inc(scores_in_psum, 1)

            def turn_probs(b, u):
                pe.wait_ge(probs_ready, b * 8 + u + 1)
                if u >= 2:
                    pe.wait_ge(pT_ready, b * 8 + u - 1)
                for j in range(J):
                    last = pe.transpose(pt_bank[u % 2][0:KW, j * QH:(j + 1) * QH], probs[:, u, j, :], T["ident"][0:QH, 0:QH])
                last.then_inc(pT_in_psum, 1)

            def weigh_values(b, u, par):
                h, c = divmod(u, KC)
                pe.wait_ge(pT_ready, b * 8 + u + 1)
                if u == 0:
                    pe.wait_ge(v_ready, b * 2 + 2)
                for j in range(J):
                    last = pe.matmul(av_bank[h][HD * j:HD * (j + 1), c * QH:(c + 1) * QH],
                                     v_tok[par][:, h, P * c + HD * j:P * c + HD * (j + 1)], probsT[u % 2][:, j, :],
                                     start=True, stop=True)
                last.then_inc(av_in_psum, 1)

            def project_out(b, h, last):
                pe.wait_ge(attnT_ready, b * 2 + h + 1)
                if last:
                    pe.wait_ge(out_added, b * 2 + 1 + h)
                else:
                    pe.wait_ge(v_ready, b * 2 + 3 + h)
                for c in range(KC):
                    mm = pe.matmul(proj_bank[h][0:QH, :], attnT[h][:, c, :], T["wproj"][:, c, :],
                                   start=(c == 0), stop=(c == KC - 1))
                mm.then_inc(out_in_psum, 1)

            def step(b, par, last=False):
                if not last:
                    transposes(b + 1, 1 - par)
                for u in range(UNITS):
                    scores(b, u)
                    if not last:
                        project_qk(b + 1, u)
                if not last:
                    project_v(b + 1, 0)
                    project_v(b + 1, 1)
                turn_probs(b, 0)
                for u in range(1, UNITS):
                    turn_probs(b, u)
                    weigh_values(b, u - 1, par)
                weigh_values(b, UNITS - 1, par)
                for h in range(2):
                    project_out(b, h, last)

            transposes(0, 0)
            for n in range(2 * KC):
                project_qk(0, n)
            project_v(0, 0)
            project_v(0, 1)
            steps(pe, step)

        @block.scalar
        def _(act):
            def turn_x(b):
                for h in range(2):
                    act.wait_ge(xT_in_psum, b * 2 + h + 1)
                    act.activation(xT[:, :, h * QH:(h + 1) * QH],
                                   proj_bank[h][:, 0:KC * QH].rearrange("p (k q) -> p k q", k=KC), ACT.Copy).then_inc(xT_ready, 1)

            def high(b, n):
                act.wait_ge(qk_in_psum, b * 8 + n + 1)
                if n == 0 and not (isinstance(b, int) and b == 0):
                    act.wait_ge(q_stacked, b * 256)
                    act.wait_ge(k_stacked, b * 256)
                act.activation(qk_hi[:, n, :], proj_bank[n % 2][:, 0:N], ACT.Copy).then_inc(qk_hi_ready, 1)

            def values(b, par):
                for w in range(2):
                    act.wait_ge(v_in_psum, b * 2 + w + 1)
                    act.activation(v_tok[par][:, w, :], proj_bank[w][0:KW, :], ACT.Copy).then_inc(v_ready, 1)

            def exps(b, u):
                act.wait_ge(max_ready, b * 8 + u + 1)
                for j in range(J):
                    last = act.activation(probs[:, u, j, :], probs[:, u, j, :], ACT.Exp, bias=neg_max[:, u, j:j + 1],
                                          scale=SCALE, accum_out=row_sum[:, u, j:j + 1])
                last.then_inc(exp_ready, 1)

            def attn_out(b, h):
                act.wait_ge(av_in_psum, b * 8 + KC * h + KC)
                act.wait_ge(out_added, b * 2 + 1 + h)
                act.activation(attnT[h][:], av_bank[h][:, 0:KC * QH].rearrange("p (k q) -> p k q", k=KC), ACT.Copy).then_inc(attnT_ready, 1)

            def step(b, par, last=False):
                if not last:
                    turn_x(b + 1)
                for u in range(UNITS):
                    if not last:
                        high(b + 1, u)
                    exps(b, u)
                if not last:
                    values(b + 1, 1 - par)
                for h in range(2):
                    attn_out(b, h)

            turn_x(0)
            for n in range(2 * KC):
                high(0, n)
            values(0, 0)
            steps(act, step)

        @block.vector
        def _(dve):
            def low(b, n):
                dve.wait_ge(qk_hi_ready, b * 8 + n + 1)
                dve.tensor_tensor(qk_lo[:, n, :], proj_bank[n % 2][:, 0:N], qk_hi[:, n, :], ALU.subtract).then_inc(qk_lo_ready, 1)

            def mask_and_max(b, u):
                h = u // KC
                for j in range(J):
                    last = dve.tensor_tensor_reduce(probs[:, u, j, :], score_bank[u % 2][0:QH, j * KW:(j + 1) * KW],
                                                    T["band"][:, h, :], 1.0, MASKED, ALU.add, ALU.max, row_max[:, u, j:j + 1])
                last.then_inc(masked_ready, 1)
                dve.wait_ge(masked_ready, b * 8 + u + 1)
                dve.tensor_scalar(neg_max[:, u, :], row_max[:, u, :], -SCALE, None, ALU.mult).then_inc(max_ready, 1)

            def invert(b, u):
                dve.wait_ge(exp_ready, b * 8 + u + 1)
                dve.reciprocal(inv_sum[:, u, :], row_sum[:, u, :]).then_inc(inv_ready, 1)

            def copy_pT(b, u):
                dve.wait_ge(pT_in_psum, b * 8 + u + 1)
                if u >= 2:
                    dve.wait_ge(av_in_psum, b * 8 + u - 1)
                dve.tensor_copy(probsT[u % 2][:].rearrange("k j q -> k (j q)"), pt_bank[u % 2][0:KW, 0:J * QH]).then_inc(pT_ready, 1)

            def add_out(b, h):
                dve.wait_ge(out_in_psum, b * 2 + h + 1)
                r = T["resid"][:, bass.ds(b * 2 + h, 1), :].rearrange("q a c -> q (a c)")
                dve.tensor_tensor(r, proj_bank[h][0:QH, :], r, ALU.add).then_inc(out_added, 1)
                dve.wait_ge(out_added, b * 2 + h + 3)
                dve.memset(waited[:], 0.0)
                dve.bn_stats(T["stats"][:, bass.ds(b * 2 + h, 1), :].rearrange("q a c -> q (a c)"), r)

            def step(b, par, last=False):
                for u in range(UNITS):
                    dve.wait_ge(scores_in_psum, b * 8 + u + 1)
                    if not last:
                        low(b + 1, u)
                    mask_and_max(b, u)
                    if u >= 1:
                        invert(b, u - 1)
                invert(b, UNITS - 1)
                for u in range(UNITS):
                    copy_pT(b, u)
                for h in range(2):
                    add_out(b, h)

            dve.memset(waited[:], 0.0).then_inc(out_added, 2)
            dve.wait_ge(bias_added, 1)
            for n in range(2 * KC):
                low(0, n)
            steps(dve, step)

        @block.gpsimd
        def _(pool):
            pool.tensor_tensor(T["resid"][:], T["resid"][:], T["bias_row"][:].rearrange("q (a c) -> q a c", a=1).broadcast_to([QH, 2 * B, C]), ALU.add).then_inc(bias_added, 1)

            def step(b, par, last=False):
                for u in range(UNITS):
                    pool.wait_ge(inv_ready, b * 8 + u + 1)
                    pool.tensor_tensor(probs[:, u], probs[:, u],
                                       inv_sum[:, u].rearrange("q (j a) -> q j a", a=1).broadcast_to([QH, J, KW]), ALU.mult).then_inc(probs_ready, 1)
            steps(pool, step)


def normalise_and_turn(nc, S, T, name, bias=None, router=False):
    B, N, C, QH = S["B"], S["N"], S["C"], S["QH"]
    KC = C // P
    ROWS = 2 * B
    with ExitStack() as ctx:
        def sb(n, shape, dt=F32):
            return ctx.enter_context(nc.sbuf_tensor(f"{name}_{n}", shape, dt))

        def sem(n):
            return ctx.enter_context(nc.semaphore(f"{name}_{n}"))

        turn_bank = [ctx.enter_context(nc.psum_tensor(f"{name}_bank{i}", [P, 512], F32)) for i in range(2)]
        if router:
            gate_w = sb("gate_w", [P, KC, S["E"]])
            logit_bank = ctx.enter_context(nc.psum_tensor(f"{name}_logits", [P, ROWS, S["E"]], F32))
        x_norm = [sb(f"x_norm{i}", [QH, C]) for i in range(2)]
        xT_tile = [sb(f"xT_tile{i}", [P, KC, QH]) for i in range(2)]
        std = sb("std", [QH, ROWS])
        rstd = sb("rstd", [QH, ROWS])
        eps = sb("eps", [QH, 1])
        mean_var, stats = T["mean_var"], T["stats"]

        bias_loaded = sem("bias_loaded")
        eps_set = sem("eps_set")
        var_ready = sem("var_ready")
        std_ready = sem("std_ready")
        rstd_ready = sem("rstd_ready")
        logits_in_psum = sem("logits_in_psum")
        norm_ready = sem("norm_ready")
        turned = sem("turned")
        xT_copied = sem("xT_copied")
        xT_stored = sem("xT_stored")
        tiles_free = sem("tiles_free")
        resid_set = sem("resid_set")
        block = ctx.enter_context(nc.Block())

        @block.sync
        def _(sp):
            for freed in (turned, xT_copied, resid_set, tiles_free):
                sp.sem_inc(freed, 2)
            if router:
                sp.dma_start(gate_w[:], S["gate_w"].rearrange("(k p) e -> p k e", p=P)).then_inc(bias_loaded, 16)
                return
            sp.dma_start(T["bias_row"][:], bias.rearrange("(a n) -> a n", a=1).broadcast_to([QH, C])).then_inc(bias_loaded, 16)
            with sp.Fori(0, ROWS // 2) as pair:
                for i in range(2):
                    r = pair * 2 + i
                    sp.wait_ge(xT_copied, r + 3)
                    sp.dma_start(S["xT"][bass.ds(r, 1)].rearrange("a p k q -> (a p) k q"), xT_tile[i][:]).then_inc(xT_stored, 16)
                sp.wait_ge(xT_stored, pair * 32 + 32)
                sp.sem_inc(tiles_free, 2)

        @block.vector
        def _(dve):
            dve.memset(eps[:], LN_EPS).then_inc(eps_set, 1)
            for r in range(ROWS):
                last = dve.bn_aggr(mean_var[:, r, :], stats[:, r, :])
            last.then_inc(var_ready, 1)
            dve.wait_ge(std_ready, 1)
            dve.reciprocal(rstd[:], std[:]).then_inc(rstd_ready, 1)
            dve.wait_ge(rstd_ready, 1)
            dve.tensor_copy(mean_var[:, :, 1], rstd[:]).then_inc(rstd_ready, 1)
            dve.wait_ge(rstd_ready, 2)
            with dve.Fori(0, ROWS // 2) as pair:
                for i in range(2):
                    r = pair * 2 + i
                    dve.wait_ge(turned, r + 1)
                    dve.wait_ge(resid_set, r + 1)
                    dve.tensor_scalar(x_norm[i][:], T["resid"][:, bass.ds(r, 1), :].rearrange("q a c -> q (a c)"),
                                      mean_var[:, bass.ds(r, 1), 0], mean_var[:, bass.ds(r, 1), 1],
                                      ALU.subtract, ALU.mult).then_inc(norm_ready, 1)
            if router:
                dve.wait_ge(logits_in_psum, ROWS)
                dve.tensor_copy(T["logits"][:], logit_bank[0:QH])

        @block.scalar
        def _(act):
            act.wait_ge(eps_set, 1)
            act.wait_ge(var_ready, 1)
            act.activation(std[:], mean_var[:, :, 1], ACT.Sqrt, bias=eps[:]).then_inc(std_ready, 1)
            with act.Fori(0, ROWS // 2) as pair:
                for i in range(2):
                    r = pair * 2 + i
                    act.wait_ge(turned, r + 3)
                    if i == 0 and not router:
                        act.wait_ge(tiles_free, pair * 2 + 2)
                    act.activation(xT_tile[i][:],
                                   turn_bank[i][:, 0:KC * QH].rearrange("p (k q) -> p k q", k=KC), ACT.Copy).then_inc(xT_copied, 1)

        @block.tensor
        def _(pe):
            if router:
                pe.wait_ge(bias_loaded, 16)
            with pe.Fori(0, ROWS // 2) as pair:
                for i in range(2):
                    r = pair * 2 + i
                    pe.wait_ge(norm_ready, r + 1)
                    pe.wait_ge(xT_copied, r + 1)
                    for k in range(KC):
                        last = pe.transpose(turn_bank[i][:, k * QH:(k + 1) * QH], x_norm[i][:, k * P:(k + 1) * P], T["ident"][0:QH, 0:QH])
                    last.then_inc(turned, 1)
                    if router:
                        pe.wait_ge(xT_copied, r + 3)
                        for k in range(KC):
                            mm = pe.matmul(logit_bank[0:QH, bass.ds(r, 1), :].rearrange("q a e -> q (a e)"), xT_tile[i][:, k, :], gate_w[:, k, :],
                                           start=(k == 0), stop=(k == KC - 1))
                        mm.then_inc(logits_in_psum, 1)

        @block.gpsimd
        def _(pool):
            if not router:
                pool.wait_ge(bias_loaded, 16)
            with pool.Fori(0, ROWS // 2) as pair:
                for i in range(2):
                    r = pair * 2 + i
                    pool.wait_ge(norm_ready, r + 1)
                    row = T["resid"][:, bass.ds(r, 1), :].rearrange("q a c -> q (a c)")
                    if router:
                        pool.tensor_copy(row, x_norm[i][:]).then_inc(resid_set, 1)
                    else:
                        pool.tensor_tensor(row, x_norm[i][:], T["bias_row"][:], ALU.add).then_inc(resid_set, 1)


class Uses:

    def __init__(self, B):
        self.prologue = [("ctx", t) for t in range(6)] + ["k0", "k1", "q", "next k0", "next k1", "next q"]
        self.kinds = {k: self.batch(k) for k in ("first", "mid", "last")}
        self.B = B
        self.tail = [("out", 0), ("out", 1)]

    @staticmethod
    def chunk(kind, c):
        uses = ["m"]
        if c == 0:
            uses += [("v", t) for t in range(6)]
        if c in (1, 3) and kind != "first":
            uses.append(("out", c // 2))
        if c == 2 and kind != "last":
            uses += [("ctx", t) for t in range(6)]
        if not (c >= 2 and kind == "last"):
            uses += ["k0", "k1", "q"]
        return uses

    def batch(self, kind):
        return [(c, u) for c in range(4) for u in self.chunk(kind, c)]

    def find(self, b, kind, c, what):
        if kind == "prologue":
            i = self.prologue.index(what)
            return i % 2, i // 2 + 1
        first = len(self.prologue)
        if kind == "tail":
            i = first + len(self.kinds["first"]) + (self.B - 2) * len(self.kinds["mid"]) + len(self.kinds["last"]) + what
            return i % 2, i // 2 + 1
        i = self.kinds[kind].index((c, what))
        if kind == "first":
            i += first
            return i % 2, i // 2 + 1
        a, m = first + len(self.kinds["first"]), len(self.kinds["mid"])
        assert a % 2 == 0 and m % 2 == 0
        return i % 2, (b - 1) * (m // 2) + (a // 2 + i // 2 + 1)


def cross_attention(nc, S, T):
    B, N, C, HD, QH = (S[k] for k in ("B", "N", "C", "HD", "QH"))
    NK = S["ctx"].shape[1]
    KC = C // P
    J = P // HD
    KT = 6
    KR = NK // KT
    KH = 376
    KP = 2 * KH
    HALF = NK // 2
    R3 = 3 * HD
    SCALE = HD ** -0.5
    RING = 3
    UT = J * KT // 2
    SPREAD = (1, 3, 5, 7, 9, 11)
    uses = Uses(B)
    with ExitStack() as ctx:
        def sb(name, shape, dt=F32):
            return ctx.enter_context(nc.sbuf_tensor(f"b_{name}", shape, dt))

        def sem(name):
            return ctx.enter_context(nc.semaphore(f"b_{name}"))

        s_bank = ctx.enter_context(nc.psum_tensor("b_scores", [P, 2, 512], F32))
        st_bank = ctx.enter_context(nc.psum_tensor("b_scoresT", [P, RING, 512], F32))
        av_bank = ctx.enter_context(nc.psum_tensor("b_av", [P, 512], F32))
        proj_bank = [ctx.enter_context(nc.psum_tensor(f"b_proj{i}", [P, 512], F32)) for i in range(2)]

        wq, wk, wv, wo = (sb(n, [P, KC, C]) for n in ("wq", "wk", "wv", "wo"))
        bq_col, bk_col = sb("bq_col", [P, KC]), sb("bk_col", [P, KC])
        bv_row = sb("bv_row", [P, C])
        ones = sb("ones", [P, HD])
        ident_r = sb("ident_r", [P, P], F32R)
        ctx_tok = sb("ctx_tok", [KR, KT, C])
        ctxT = sb("ctxT", [P, KC, NK])
        k_hi, k_lo = sb("k_hi", [P, NK], F32R), sb("k_lo", [P, NK], F32R)
        q_hi, q_lo = sb("q_hi", [P, N], F32R), sb("q_lo", [P, N], F32R)
        k_stack = [sb(f"k_stack{i}", [P, J, KP], F32R) for i in range(2)]
        q_stack = [sb(f"q_stack{i}", [P, J, N], F32R) for i in range(2)]
        xT = [sb(f"xT{i}", [P, 2, KC, QH]) for i in range(2)]
        mask_int = sb("mask_int", [QH, 2, NK], I32)
        mask_bias = [sb(f"mask_bias{i}", [QH, 2, KP], F32R) for i in range(2)]
        row_max = [sb(f"row_max{i}", [QH, J * 2]) for i in range(2)]
        neg_max = sb("neg_max", [QH, J * 2], F32R)
        neg_max_rows = sb("neg_max_rows", [J * 2, QH])
        v_tok = sb("v_tok", [KR, KT, C])
        probsT = sb("probsT", [KR, J, KT, N])
        half_sum = sb("half_sum", [KR, 3, N])
        key_sum = sb("key_sum", [KR, J, N])
        inv_den = sb("inv_den", [P, N])
        attnT = [sb(f"attnT{i}", [P, KC, N]) for i in range(2)]
        waited = sb("waited", [QH, 5])

        w_loaded = sem("w_loaded")
        set_up = sem("set_up")
        ctx_loaded = sem("ctx_loaded")
        xT_loaded = sem("xT_loaded")
        mask_loaded = sem("mask_loaded")
        mask_ready = sem("mask_ready")
        filled = [sem(f"filled{i}") for i in range(2)]
        freed = [sem(f"freed{i}") for i in range(2)]
        hi_ready = sem("hi_ready")
        stacked = [sem(f"stacked{j}") for j in range(J)]
        s_in_psum = sem("s_in_psum")
        max_ready = sem("max_ready")
        neg_ready = sem("neg_ready")
        max_placed = sem("max_placed")
        st_in_psum = sem("st_in_psum")
        exp_ready = sem("exp_ready")
        halves_added = sem("halves_added")
        sum_ready = sem("sum_ready")
        av_in_psum = sem("av_in_psum")
        inv_ready = sem("inv_ready")
        attnT_ready = sem("attnT_ready")

        block = ctx.enter_context(nc.Block())

        def steps(eng, chunk):
            def batch(b, kind, par):
                for c in range(KC):
                    one, two = ((b, c + i, par) if c + i < KC else (b + 1, c + i - KC, 1 - par) if kind != "last" else None
                                for i in (1, 2))
                    chunk(b, c, kind, par, one, two)
            batch(0, "first", 0)
            with eng.Fori(0, B // 2 - 1) as pair:
                batch(pair * 2 + 1, "mid", 1)
                batch(pair * 2 + 2, "mid", 0)
            batch(B - 1, "last", 1)

        def wait_free(pe, b, kind, c, what):
            i, n = uses.find(b, kind, c, what)
            if not (isinstance(n, int) and n == 1):
                pe.wait_ge(freed[i], n - 1)
            return i

        def wait_filled(eng, b, kind, c, what):
            i, n = uses.find(b, kind, c, what)
            eng.wait_ge(filled[i], n)
            return i

        def wait_freed(eng, b, kind, c, whats):
            for what in whats:
                i, n = uses.find(b, kind, c, what)
                eng.wait_ge(freed[i], n)

        @block.sync
        def _(sp):
            def load_ctx(b):
                sp.dma_start(ctx_tok[:], S["ctx"].rearrange("b (t p) c -> b p t c", p=KR)[bass.ds(b, 1)].rearrange("a p t c -> (a p) t c")).then_inc(ctx_loaded, 16)

            def load_xT(b, par):
                sp.dma_start(xT[par][:].rearrange("p h k q -> p h (k q)"),
                             S["xT"].rearrange("(b h) p k q -> b p h (k q)", h=2)[bass.ds(b, 1)].rearrange("a p h n -> (a p) h n")).then_inc(xT_loaded, 16)

            def load_mask(b):
                sp.dma_start(mask_int[:], S["mask"].rearrange("b (h q) k -> b q h k", q=QH)[bass.ds(b, 1)].rearrange("a q h k -> (a q) h k")).then_inc(mask_loaded, 16)

            def stack(i, kind, c, bk, prefix=""):
                wait_freed(sp, bk, kind, c, (prefix + "q",))
                for j in range(J):
                    for dst, order, n in ((q_stack, (q_hi, q_hi, q_lo), N), (k_stack, (k_hi, k_lo, k_hi), NK)):
                        for r, src in enumerate(order):
                            sp.dma_start(dst[i][HD * r:HD * r + HD, j, 0:n].bitcast(F32),
                                         src[HD * j:HD * j + HD, :].bitcast(F32)).then_inc(stacked[j], 16)

            def chunk(b, c, kind, par, one, two):
                if two is not None:
                    stack(c % 2, kind, c, b)
                if c == 0 and kind != "last":
                    load_ctx(b + 1)
                    load_xT(b + 1, 1 - par)
                    load_mask(b + 1)

            for dst, name in ((wk, "Wk"), (wq, "Wq"), (wv, "Wv"), (wo, "Wo")):
                sp.dma_start(dst[:], S[name].rearrange("(k p) n -> p k n", p=P)).then_inc(w_loaded, 16)
            sp.dma_start(bv_row[:], S["bv"].rearrange("(a n) -> a n", a=1).broadcast_to([P, C])).then_inc(w_loaded, 16)
            for dst, name in ((bq_col, "bq"), (bk_col, "bk")):
                with nc.allow_non_contiguous_dma(reason="two columns of 4 x 128 values"):
                    sp.dma_start(dst[:], S[name].rearrange("(k p) -> p k", p=P)).then_inc(w_loaded, 16)
            load_ctx(0)
            load_mask(0)
            load_xT(0, 0)
            stack(0, "prologue", 0, 0)
            stack(1, "prologue", 0, 0, "next ")
            steps(sp, chunk)

        @block.tensor
        def _(pe):
            def turn_ctx(b, kind, c, bk):
                pe.wait_ge(ctx_loaded, b * 16 + 16)
                for t in range(KT):
                    i = wait_free(pe, bk, kind, c, ("ctx", t))
                    for k in range(KC):
                        mm = pe.transpose(proj_bank[i][:, k * KR:(k + 1) * KR], ctx_tok[:, t, k * P:(k + 1) * P], T["ident"][0:KR, 0:KR])
                    mm.then_inc(filled[i], 1)

            def project_k(cn, kind, c, half, bk, prefix=""):
                i = wait_free(pe, bk, kind, c, f"{prefix}k{half}")
                if half == 0 and cn == 0:
                    wait_freed(pe, bk, kind, c, (("ctx", KT - 2), ("ctx", KT - 1)))
                for k in range(KC):
                    mm = pe.matmul(proj_bank[i][:, 0:HALF], wk[:, k, cn * P:(cn + 1) * P], ctxT[:, k, half * HALF:(half + 1) * HALF],
                                   start=(k == 0), stop=(k == KC - 1))
                mm.then_inc(filled[i], 1)

            def project_q(b, cn, kind, c, bk, xpar, prefix=""):
                i = wait_free(pe, bk, kind, c, prefix + "q")
                if cn == 0:
                    pe.wait_ge(xT_loaded, b * 16 + 16)
                for k in range(KC):
                    mm = pe.matmul(proj_bank[i][:, 0:N], wq[:, k, cn * P:(cn + 1) * P], xT[xpar][:, :, k, :],
                                   start=(k == 0), stop=(k == KC - 1))
                mm.then_inc(filled[i], 1)

            def project_v(b, kind, c, t):
                i = wait_free(pe, b, kind, c, ("v", t))
                for k in range(KC):
                    mm = pe.matmul(proj_bank[i][0:KR, :], ctxT[:, k, t * KR:(t + 1) * KR], wv[:, k, :],
                                   start=(k == 0), stop=(k == KC - 1))
                mm.then_inc(filled[i], 1)

            def project_out(b, h, kind, c, what, par, bk):
                i = wait_free(pe, bk, kind, c, what)
                if h == 0:
                    pe.wait_ge(attnT_ready, b * KC + KC)
                for k in range(KC):
                    mm = pe.matmul(proj_bank[i][0:QH, :], attnT[par][:, k, h * QH:(h + 1) * QH], wo[:, k, :],
                                   start=(k == 0), stop=(k == KC - 1))
                mm.then_inc(filled[i], 1)

            def turn_max(b, kind, c):
                i = wait_free(pe, b, kind, c, "m")
                pe.wait_ge(neg_ready, b * KC + c + 1)
                pe.transpose(proj_bank[i][0:J * 2, 0:QH], neg_max[:].bitcast(F32), T["ident"][0:QH, 0:QH]).then_inc(filled[i], 1)

            def scores(b, c, u):
                g = b * KC + c
                j, h = divmod(u, 2)
                if h == 0:
                    pe.wait_ge(stacked[j], g * 96 + 96)
                if not (isinstance(g, int) and g == 0 and u == 0):
                    pe.wait_ge(max_ready, g * 8 + u)
                for a in range(2):
                    mm = pe.matmul(s_bank[0:QH, a, 0:KH], q_stack[c % 2][0:R3, j, h * QH:(h + 1) * QH],
                                   k_stack[c % 2][0:R3, j, a * KH:(a + 1) * KH], start=True, stop=True)
                mm.then_inc(s_in_psum, 1)

            def scoresT(b, c, r, par):
                g = b * KC + c
                j = r // 3
                if r == 0:
                    pe.wait_ge(max_placed, g * 16 + 16)
                if not (isinstance(g, int) and g == 0 and r < RING):
                    pe.wait_ge(exp_ready, g * UT + r - RING + 1)
                for a in range(2):
                    t = 2 * (r % 3) + a
                    out = st_bank[0:KR, r % RING, a * N:(a + 1) * N]
                    pe.matmul(out, k_stack[c % 2][:, j, t * KR:(t + 1) * KR], q_stack[c % 2][:, j, :], start=True, stop=False)
                    for h in range(2):
                        mm = pe.matmul(st_bank[0:KR, r % RING, a * N + h * QH:a * N + (h + 1) * QH],
                                       mask_bias[par][:, h, t * KR:(t + 1) * KR], ident_r[0:QH, 0:QH], start=False, stop=(h == 1))
                mm.then_inc(st_in_psum, 1)

            def weigh_values(g, c, v_uses, between=None):
                pe.wait_ge(exp_ready, g * UT + UT)
                if not (isinstance(g, int) and g == 0):
                    pe.wait_ge(attnT_ready, g)
                if v_uses is not None:
                    wait_freed(pe, *v_uses, (("v", KT - 2), ("v", KT - 1)))
                for t in range(KT):
                    for j in range(J):
                        pe.matmul(av_bank[HD * j:HD * (j + 1), 0:N], v_tok[:, t, P * c + HD * j:P * c + HD * (j + 1)],
                                  probsT[:, j, t, :], start=(t == 0), stop=(t == KT - 1), skip_group_check=True)
                    if t == 1 and between is not None:
                        turn_max(*between)
                pe.wait_ge(sum_ready, g * J + J)
                for j in range(J):
                    mm = pe.matmul(av_bank[HD * j:HD * (j + 1), 256:256 + N], ones[0:KR, :], key_sum[:, j, :],
                                   start=True, stop=True, skip_group_check=True)
                mm.then_inc(av_in_psum, 1)

            def chunk(b, c, kind, par, one, two):
                g = b * KC + c
                if not (kind == "first" and c == 0):
                    weigh_values(g - 1, (c - 1) % KC, (b, kind, 0) if c == 1 else None, (b, kind, c))
                else:
                    turn_max(b, kind, c)
                if c == 0:
                    project_v(b, kind, c, 0)
                    project_v(b, kind, c, 1)
                if c in (1, 3) and kind != "first":
                    project_out(b - 1, c // 2, kind, c, ("out", c // 2), 1 - par, b)
                if c == 2 and kind != "last":
                    turn_ctx(b + 1, kind, c, b)
                for r in range(UT):
                    scoresT(b, c, r, par)
                    if r in SPREAD and one is not None:
                        scores(one[0], one[1], SPREAD.index(r))
                    if r % 3 == 2 and c == 0:
                        project_v(b, kind, c, 2 + r // 3)
                if two is not None:
                    project_k(two[1], kind, c, 0, b)
                if one is not None:
                    scores(one[0], one[1], 6)
                if two is not None:
                    project_k(two[1], kind, c, 1, b)
                if one is not None:
                    scores(one[0], one[1], 7)
                if two is not None:
                    project_q(two[0], two[1], kind, c, b, two[2])

            pe.wait_ge(w_loaded, 7 * 16)
            pe.wait_ge(set_up, SETUPS)
            turn_ctx(0, "prologue", 0, 0)
            project_k(0, "prologue", 0, 0, 0)
            project_k(0, "prologue", 0, 1, 0)
            project_q(0, 0, "prologue", 0, 0, 0)
            project_k(1, "prologue", 0, 0, 0, "next ")
            project_k(1, "prologue", 0, 1, 0, "next ")
            project_q(0, 1, "prologue", 0, 0, 0, "next ")
            for u in range(2 * J):
                scores(0, 0, u)
            steps(pe, chunk)
            weigh_values(B * KC - 1, KC - 1, None)
            for h in range(2):
                project_out(B - 1, h, "tail", 0, h, 1, 0)

        @block.scalar
        def _(act):
            def copy_ctx(kind, c, t, bk):
                i = wait_filled(act, bk, kind, c, ("ctx", t))
                act.activation(ctxT[:, :, t * KR:(t + 1) * KR],
                               proj_bank[i][:, 0:KC * KR].rearrange("p (k q) -> p k q", k=KC), ACT.Copy).then_inc(freed[i], 1)

            def high(b, cn, kind, c, bk, prefix=""):
                g = b * KC + cn
                for n, what in enumerate(("k0", "k1", "q")):
                    i = wait_filled(act, bk, kind, c, prefix + what)
                    if n == 0 and not (isinstance(g, int) and g == 0):
                        for j in range(J):
                            act.wait_ge(stacked[j], g * 96)
                    if what == "q":
                        out, src, bias = q_hi[:], proj_bank[i][:, 0:N], bq_col
                    else:
                        out, src, bias = k_hi[:, n * HALF:(n + 1) * HALF], proj_bank[i][:, 0:HALF], bk_col
                    act.activation(out, src, ACT.Identity, bias=bias[:, cn:cn + 1]).then_inc(hi_ready, 1)

            def exps(b, c):
                g = b * KC + c
                for r in range(UT):
                    j, a = divmod(r, 3)
                    act.wait_ge(st_in_psum, g * UT + r + 1)
                    if r == 0 and not (isinstance(g, int) and g == 0):
                        act.wait_ge(av_in_psum, g)
                    act.activation(probsT[:, j, 2 * a:2 * a + 2, :].rearrange("k t q -> k (t q)"), st_bank[0:KR, r % RING, 0:2 * N],
                                   ACT.Exp, scale=SCALE).then_inc(exp_ready, 1)

            def chunk(b, c, kind, par, one, two):
                wait_freed(act, b, kind, c, ("m",))
                act.dma_start(q_stack[c % 2][R3:R3 + 1, :, :].bitcast(F32).rearrange("a j (h q) -> a (j h) q", h=2),
                               neg_max_rows[:]).then_inc(max_placed, 16)
                if c == 2 and kind != "last":
                    for t in range(KT):
                        copy_ctx(kind, c, t, b)
                exps(b, c)
                if two is not None:
                    high(two[0], two[1], kind, c, b)

            act.wait_ge(w_loaded, 7 * 16)
            for t in range(KT):
                copy_ctx("prologue", 0, t, 0)
            high(0, 0, "prologue", 0, 0)
            high(0, 1, "prologue", 0, 0, "next ")
            steps(act, chunk)

        @block.vector
        def _(dve):
            def low(b, cn, kind, c, bk, n, prefix=""):
                g = b * KC + cn
                what = ("k0", "k1", "q")[n]
                i, _ = uses.find(bk, kind, c, prefix + what)
                dve.wait_ge(hi_ready, g * 3 + n + 1)
                if what == "q":
                    out, src, bias, hi = q_lo[:], proj_bank[i][:, 0:N], bq_col, q_hi[:]
                else:
                    out, src, bias, hi = (k_lo[:, n * HALF:(n + 1) * HALF], proj_bank[i][:, 0:HALF], bk_col,
                                          k_hi[:, n * HALF:(n + 1) * HALF])
                dve.scalar_tensor_tensor(out=out, in0=src, scalar=bias[:, cn:cn + 1], in1=hi.bitcast(F32),
                                         op0=ALU.add, op1=ALU.subtract).then_inc(freed[i], 1)

            def negate(b, c):
                g = b * KC + c
                dve.wait_ge(max_ready, g * 8 + 8)
                dve.tensor_scalar(neg_max[:], row_max[c % 2][:], -1.0, None, ALU.mult).then_inc(neg_ready, 1)

            def copy_rows(b, kind, c):
                g = b * KC + c
                i = wait_filled(dve, b, kind, c, "m")
                if not (isinstance(g, int) and g == 0):
                    dve.wait_ge(max_placed, g * 16)
                dve.tensor_copy(neg_max_rows[:], proj_bank[i][0:2 * J, 0:QH]).then_inc(freed[i], 1)

            def values(b, kind, t):
                i = wait_filled(dve, b, kind, 0, ("v", t))
                dve.tensor_tensor(v_tok[:, t, :], proj_bank[i][0:KR, :], bv_row[0:KR, :], ALU.add).then_inc(freed[i], 1)

            def add_out(b, h, kind, c, what, bk):
                i = wait_filled(dve, bk, kind, c, what)
                r = T["resid"][:, bass.ds(b * 2 + h, 1), :].rearrange("q a c -> q (a c)")
                dve.tensor_tensor(r, proj_bank[i][0:QH, :], r, ALU.add).then_inc(freed[i], 1)
                dve.wait_ge(freed[i], uses.find(bk, kind, c, what)[1])
                dve.memset(waited[:, 4:5], 0.0)
                dve.bn_stats(T["stats"][:, bass.ds(b * 2 + h, 1), :].rearrange("q a c -> q (a c)"), r)

            def make_mask(b, par):
                dve.wait_ge(mask_loaded, b * 16 + 16)
                dve.tensor_scalar(mask_bias[par][:, :, 0:NK], mask_int[:], 0.0, MASKED, ALU.is_equal, ALU.mult).then_inc(mask_ready, 1)

            def maxima(b, c, u, par):
                dve.wait_ge(s_in_psum, (b * KC + c) * 8 + u + 1)
                dve.memset(waited[:, u % 4:u % 4 + 1], 0.0)
                h = u % 2
                pair = s_bank[0:QH, :, 0:KH]
                dve.tensor_tensor_reduce(pair, pair,
                                         mask_bias[par][:, h, :].bitcast(F32).rearrange("q (a k) -> q a k", a=2), 1.0, -3.0e38,
                                         ALU.add, ALU.max, row_max[c % 2][:, u:u + 1]).then_inc(max_ready, 1)

            def normalise(g, c, par):
                dve.wait_ge(av_in_psum, g + 1)
                dve.reciprocal(inv_den[:], av_bank[:, 256:256 + N]).then_inc(inv_ready, 1)
                dve.wait_ge(inv_ready, g + 1)
                dve.tensor_tensor(attnT[par][:, c, :], av_bank[:, 0:N], inv_den[:], ALU.mult).then_inc(attnT_ready, 1)

            def chunk(b, c, kind, par, one, two):
                negate(b, c)
                copy_rows(b, kind, c)
                if not (kind == "first" and c == 0):
                    normalise(b * KC + c - 1, (c - 1) % KC, 1 - par if c == 0 else par)
                if c == 0:
                    values(b, kind, 0)
                    values(b, kind, 1)
                if c in (1, 3) and kind != "first":
                    add_out(b - 1, c // 2, kind, c, ("out", c // 2), b)
                if c == 2 and kind != "last":
                    make_mask(b + 1, 1 - par)
                for r in range(UT):
                    if r in SPREAD and one is not None:
                        maxima(one[0], one[1], SPREAD.index(r), one[2])
                    if r % 3 == 2 and c == 0:
                        values(b, kind, 2 + r // 3)
                for n in range(2):
                    if two is not None:
                        low(two[0], two[1], kind, c, b, n)
                    if one is not None:
                        maxima(one[0], one[1], 6 + n, one[2])
                if two is not None:
                    low(two[0], two[1], kind, c, b, 2)

            for i in range(2):
                dve.memset(k_stack[i][R3:P].bitcast(F32), 1.0).then_inc(set_up, 1)
                dve.memset(k_stack[i][0:R3, :, NK:KP].bitcast(F32), 0.0).then_inc(set_up, 1)
                dve.memset(q_stack[i][R3:P].bitcast(F32), 0.0).then_inc(set_up, 1)
                dve.memset(mask_bias[i][:, :, NK:KP].bitcast(F32), MASKED).then_inc(set_up, 1)
            dve.memset(ones[:], 1.0).then_inc(set_up, 1)
            dve.tensor_copy(ident_r[:], T["ident"][:]).then_inc(set_up, 1)
            make_mask(0, 0)
            dve.wait_ge(w_loaded, 7 * 16)
            for n in range(3):
                low(0, 0, "prologue", 0, 0, n)
            for n in range(3):
                low(0, 1, "prologue", 0, 0, n, "next ")
            for u in range(2 * J):
                maxima(0, 0, u, 0)
            steps(dve, chunk)
            normalise(B * KC - 1, KC - 1, 1)
            for h in range(2):
                add_out(B - 1, h, "tail", 0, h, 0)

        @block.gpsimd
        def _(pool):
            def chunk(b, c, kind, par, one, two):
                g = b * KC + c
                if not (isinstance(g, int) and g == 0):
                    pool.wait_ge(av_in_psum, g)
                for j in range(J):
                    n = g * J + j
                    if not (isinstance(n, int) and n == 0):
                        pool.wait_ge(sum_ready, n)
                    pool.wait_ge(exp_ready, g * UT + 3 * j + 3)
                    pool.tensor_tensor(half_sum[:], probsT[:, j, 0:3, :], probsT[:, j, 3:6, :], ALU.add).then_inc(halves_added, 1)
                    pool.wait_ge(halves_added, n * 2 + 1)
                    pool.tensor_tensor(half_sum[:, 0, :], half_sum[:, 0, :], half_sum[:, 1, :], ALU.add).then_inc(halves_added, 1)
                    pool.wait_ge(halves_added, n * 2 + 2)
                    pool.tensor_tensor(key_sum[:, j, :], half_sum[:, 0, :], half_sum[:, 2, :], ALU.add).then_inc(sum_ready, 1)
            steps(pool, chunk)


SETUPS = 10


def route(nc, S, T):
    B, N, C, QH, E = S["B"], S["N"], S["C"], S["QH"], S["E"]
    ROWS, TILES = 2 * B, S["TILES"]
    STEPS = -(-B * N // P)
    with ExitStack() as ctx:
        def sb(n, shape, dt=F32):
            return ctx.enter_context(nc.sbuf_tensor(f"r_{n}", shape, dt))

        def sem(n):
            return ctx.enter_context(nc.semaphore(f"r_{n}"))

        rank_bank = ctx.enter_context(nc.psum_tensor("r_rank", [P, ROWS, E], F32))
        total_bank = ctx.enter_context(nc.psum_tensor("r_total", [P, 512], F32))
        before = sb("before", [QH, QH])
        ones = sb("ones", [QH, QH])
        order = sb("order", [QH, E])
        thresholds = sb("thresholds", [QH, STEPS])
        earlier = sb("earlier", [QH, E, E])
        tile_no = sb("tile_no", [QH, TILES])
        prob = sb("prob", [QH, ROWS, E])
        rest = sb("rest", [QH, ROWS, E])
        work = sb("work", [QH, ROWS, E])
        pick = [sb(f"pick{i}", [QH, ROWS, E]) for i in range(2)]
        both = sb("both", [QH, ROWS, E])
        best = [sb(f"best{i}", [QH, ROWS]) for i in range(2)]
        col = sb("col", [QH, ROWS])
        col2 = sb("col2", [QH, ROWS])
        count = sb("count", [QH, E])
        over = sb("over", [QH, E, STEPS])
        tiles = sb("tiles", [QH, E])
        share = sb("share", [QH, E, E])
        first_tile = sb("first_tile", [QH, E])
        slot_f = sb("slot_f", [QH, ROWS])
        passed = sb("passed", [QH, TILES, E])
        expert_f = sb("expert_f", [QH, TILES])
        changes_f = sb("changes_f", [1, TILES])

        made = sem("made")
        step = sem("step")
        logits_less_max = sem("logits_less_max")
        exp_ready = sem("exp_ready")
        picks_ready = sem("picks_ready")
        ranks_ready = sem("ranks_ready")
        slots_ready = sem("slots_ready")
        scattered = sem("scattered")
        stored = sem("stored")
        block = ctx.enter_context(nc.Block())

        def per_row(a):
            return a.rearrange("q (r a) -> q r a", a=1).broadcast_to([QH, ROWS, E])

        def per_expert(a):
            return a.rearrange("q (a e) -> q a e", a=1).broadcast_to([QH, ROWS, E])

        @block.gpsimd
        def _(pool):
            pool.memset(before[:], 1.0).then_inc(made, 1)
            pool.memset(ones[:], 1.0).then_inc(made, 1)
            pool.memset(earlier[:], 1.0).then_inc(made, 1)
            pool.iota(order[:], pattern=[[-1, E]], base=E, channel_multiplier=0, allow_small_or_imprecise_dtypes=True).then_inc(made, 1)
            pool.iota(thresholds[:], pattern=[[P, STEPS]], base=0, channel_multiplier=0, allow_small_or_imprecise_dtypes=True).then_inc(made, 1)
            pool.iota(tile_no[:], pattern=[[1, TILES]], base=0, channel_multiplier=0, allow_small_or_imprecise_dtypes=True).then_inc(made, 1)
            pool.wait_ge(made, 6)
            pool.affine_select(out=before[:], in_=before[:], compare_op=ALU.is_gt, fill=0.0, base=0,
                               pattern=[[1, QH]], channel_multiplier=-1).then_inc(made, 1)
            pool.affine_select(out=earlier[:], in_=earlier[:], compare_op=ALU.is_gt, fill=0.0, base=0,
                               pattern=[[1, E], [-1, E]], channel_multiplier=0).then_inc(made, 1)
            pool.wait_ge(slots_ready, 1)
            for r in range(ROWS):
                for i in range(2):
                    pool.indirect_dma_start(out=S["x_rows"], out_offset=bass.IndirectOffsetOnAxis(ap=T["slot"][:, i, r:r + 1], axis=0),
                                            in_=T["resid"][:, r, :], in_offset=None).then_inc(scattered, 16)
            pool.wait_ge(scattered, 2 * ROWS * 16)

        @block.scalar
        def _(act):
            act.wait_ge(logits_less_max, 1)
            act.activation(prob[:], work[:], ACT.Exp).then_inc(exp_ready, 1)

        @block.tensor
        def _(pe):
            pe.wait_ge(made, 8)
            pe.wait_ge(picks_ready, 1)
            pe.matmul(rank_bank[0:QH].rearrange("q r e -> q (r e)"), before[:], both[:].rearrange("q r e -> q (r e)"),
                      start=True, stop=True, skip_group_check=True)
            for r in range(ROWS - 1):
                pe.matmul(rank_bank[0:QH, r + 1:ROWS, :], ones[:],
                          both[:, r:r + 1, :].broadcast_to([QH, ROWS - 1 - r, E]), start=False, stop=True,
                          skip_group_check=True)
            for r in range(ROWS):
                mm = pe.matmul(total_bank[0:QH, 0:E], ones[:], both[:, r, :], start=(r == 0), stop=(r == ROWS - 1))
            mm.then_inc(ranks_ready, 1)

        @block.vector
        def _(dve):
            done = [0]

            def then(ins):
                done[0] += 1
                ins.then_inc(step, 1)
                dve.wait_ge(step, done[0])

            def choose(source, i):
                then(dve.tensor_reduce(best[i][:], source, AX_X, ALU.max))
                then(dve.tensor_tensor(work[:], source, per_row(best[i][:]), ALU.is_equal))
                then(dve.tensor_tensor(work[:], work[:], per_expert(order[:]), ALU.mult))
                then(dve.tensor_reduce(col[:], work[:], AX_X, ALU.max))
                then(dve.tensor_tensor(pick[i][:], work[:], per_row(col[:]), ALU.is_equal))

            dve.wait_ge(made, 8)
            then(dve.tensor_reduce(col[:], T["logits"][:], AX_X, ALU.max))
            dve.tensor_tensor(work[:], T["logits"][:], per_row(col[:]), ALU.subtract).then_inc(logits_less_max, 1)
            dve.wait_ge(exp_ready, 1)
            then(dve.tensor_reduce(col[:], prob[:], AX_X, ALU.add))
            then(dve.reciprocal(col2[:], col[:]))
            then(dve.tensor_tensor(prob[:], prob[:], per_row(col2[:]), ALU.mult))
            choose(prob[:], 0)
            then(dve.scalar_tensor_tensor(out=rest[:].rearrange("q r e -> q (r e)"), in0=pick[0][:].rearrange("q r e -> q (r e)"),
                                          scalar=-4.0, in1=prob[:].rearrange("q r e -> q (r e)"), op0=ALU.mult, op1=ALU.add))
            choose(rest[:], 1)
            dve.tensor_tensor(both[:], pick[0][:], pick[1][:], ALU.add).then_inc(picks_ready, 1)
            then(dve.tensor_tensor(col[:], best[0][:], best[1][:], ALU.add))
            then(dve.reciprocal(col2[:], col[:]))
            for i in range(2):
                then(dve.tensor_tensor(T["share"][:, i, :], best[i][:], col2[:], ALU.mult))
            dve.wait_ge(ranks_ready, 1)
            then(dve.tensor_copy(count[:], total_bank[0:QH, 0:E]))
            then(dve.tensor_tensor(over[:], count[:].rearrange("q (e a) -> q e a", a=1).broadcast_to([QH, E, STEPS]),
                                   thresholds[:].rearrange("q (a s) -> q a s", a=1).broadcast_to([QH, E, STEPS]), ALU.is_gt))
            then(dve.tensor_reduce(tiles[:], over[:], AX_X, ALU.add))
            then(dve.tensor_tensor(share[:], earlier[:], tiles[:].rearrange("q (a e) -> q a e", a=1).broadcast_to([QH, E, E]), ALU.mult))
            then(dve.tensor_reduce(first_tile[:], share[:], AX_X, ALU.add))
            then(dve.tensor_scalar(count[:], first_tile[:], float(P), None, ALU.mult))
            then(dve.tensor_tensor(rest[:], rank_bank[0:QH], per_expert(count[:]), ALU.add))
            for i in range(2):
                then(dve.tensor_tensor(work[:], pick[i][:], rest[:], ALU.mult))
                then(dve.tensor_reduce(slot_f[:], work[:], AX_X, ALU.add))
                then(dve.tensor_copy(T["slot"][:, i, :], slot_f[:]))
            then(dve.tensor_tensor(passed[:], tile_no[:].rearrange("q (t a) -> q t a", a=1).broadcast_to([QH, TILES, E]),
                                   first_tile[:].rearrange("q (a e) -> q a e", a=1).broadcast_to([QH, TILES, E]), ALU.is_ge))
            then(dve.tensor_reduce(expert_f[:], passed[:, :, 1:E], AX_X, ALU.add))
            then(dve.tensor_copy(T["expert"][:, 0:TILES], expert_f[0:1, :]))
            then(dve.memset(changes_f[:], 1.0))
            then(dve.tensor_tensor(changes_f[:, 2:TILES], expert_f[0:1, 2:TILES], expert_f[0:1, 0:TILES - 2], ALU.not_equal))
            then(dve.tensor_copy(T["changes"][:, 0:TILES], changes_f[:]))
            dve.memset(col[:], 0.0).then_inc(slots_ready, 1)


def experts(nc, S, T):
    C, E, F, TILES = S["C"], S["E"], S["F"], S["TILES"]
    KC, FC = C // P, F // P
    GU = 2 * F // 512
    with ExitStack() as ctx:
        def sb(n, shape, dt=F32):
            return ctx.enter_context(nc.sbuf_tensor(f"e_{n}", shape, dt))

        def sem(n):
            return ctx.enter_context(nc.semaphore(f"e_{n}"))

        gate_bank = ctx.enter_context(nc.psum_tensor("e_gate", [P, 2, 512], F32))
        up_bank = ctx.enter_context(nc.psum_tensor("e_up", [P, 2, 512], F32))
        h_bank = [ctx.enter_context(nc.psum_tensor(f"e_h{i}", [P, 512], F32)) for i in range(2)]
        x_bank = ctx.enter_context(nc.psum_tensor("e_x", [P, 512], F32))
        y_bank = ctx.enter_context(nc.psum_tensor("e_y", [P, 512], F32))

        w_gu = [sb(f"w_gu{i}", [P, KC, 2 * F]) for i in range(2)]
        w_down = [sb(f"w_down{i}", [P, FC, C]) for i in range(2)]
        x_rows = [sb(f"x_rows{i}", [P, C]) for i in range(2)]
        xT = [sb(f"xT{i}", [P, KC, P]) for i in range(2)]
        gate = [sb(f"gate{i}", [P, F]) for i in range(2)]
        hidden = [sb(f"hidden{i}", [P, F]) for i in range(2)]
        hiddenT = sb("hiddenT", [P, FC, P])
        y_rows = [sb(f"y_rows{i}", [P, C]) for i in range(2)]

        w_gu_loaded = [sem(f"w_gu_loaded{i}") for i in range(2)]
        w_down_loaded = [sem(f"w_down_loaded{i}") for i in range(2)]
        x_loaded = [sem(f"x_loaded{i}") for i in range(2)]
        xT_in_psum = sem("xT_in_psum")
        xT_ready = sem("xT_ready")
        gu_in_psum = sem("gu_in_psum")
        silu_ready = sem("silu_ready")
        hidden_ready = sem("hidden_ready")
        hT_in_psum = sem("hT_in_psum")
        hT_ready = sem("hT_ready")
        y_in_psum = sem("y_in_psum")
        y_ready = sem("y_ready")
        y_stored = [sem(f"y_stored{i}") for i in range(2)]
        block = ctx.enter_context(nc.Block())

        def steps(eng, tile):
            tile(0, 0, 0)
            tile(1, 1, 0)
            tile(2, 0, 1)
            with eng.Fori(1, (TILES - 3) // 2) as pair:
                tile(pair * 2 + 1, 1, pair)
                tile(pair * 2 + 2, 0, pair + 1)
            tile(TILES - 2, 1, (TILES - 2) // 2)
            tile(TILES - 1, 0, (TILES - 1) // 2)

        @block.sync
        def _(sp):
            def expert_of(t):
                return sp.value_load(T["expert"][0:1, bass.ds(t, 1)], min_val=0, max_val=E - 1)

            def changes(t):
                return sp.value_load(T["changes"][0:1, bass.ds(t, 1)], min_val=0, max_val=1)

            def load_x(t, par):
                sp.dma_start(x_rows[par][:], S["x_rows"].rearrange("(t p) c -> t p c", p=P)[bass.ds(t, 1)].rearrange("a p c -> (a p) c")).then_inc(x_loaded[par], 16)

            def load_gu(e, par, cond=None):
                sp.dma_start(w_gu[par][:], S["gate_up_w"].rearrange("e (k p) n -> e p k n", p=P)[bass.ds(e, 1)].rearrange("a p k n -> (a p) k n"),
                             cond=cond).then_inc(w_gu_loaded[par], 16)

            def load_down(e, par, cond=None):
                sp.dma_start(w_down[par][:], S["down_w"].rearrange("e (k p) n -> e p k n", p=P)[bass.ds(e, 1)].rearrange("a p k n -> (a p) k n"),
                             cond=cond).then_inc(w_down_loaded[par], 16)

            def tile(t, par, turn):
                more_gu = not (isinstance(t, int) and t + 2 >= TILES)
                more_down = not (isinstance(t, int) and (t == 0 or t + 1 >= TILES))
                if more_gu:
                    e_gu, new_gu = expert_of(t + 2), changes(t + 2)
                if more_down:
                    e_down, new_down = expert_of(t + 1), changes(t + 1)
                if more_gu:
                    sp.wait_ge(gu_in_psum, t * 2 + 2)
                    load_x(t + 2, par)
                    load_gu(e_gu, par, new_gu)
                if more_down:
                    sp.wait_ge(y_in_psum, t)
                    load_down(e_down, 1 - par, new_down)

            for t in range(2):
                load_x(t, t)
                e = expert_of(t)
                load_gu(e, t)
                load_down(e, t)
            steps(sp, tile)

        @block.scalar
        def _(act):
            def silu(t, a, par):
                act.wait_ge(gu_in_psum, t * 2 + a + 1)
                act.activation(gate[par][:, a * 512:(a + 1) * 512], gate_bank[:, a, :], ACT.Silu).then_inc(silu_ready, 1)

            def tile(t, par, turn):
                first = isinstance(t, int) and t == 0
                silu(t, 0, par)
                if not first:
                    copy_hT(t - 1)
                silu(t, 1, par)
                if not first:
                    copy_y(t - 1, 1 - par, turn if par == 1 else turn - 1)
                if isinstance(t, int) and t == TILES - 1:
                    copy_hT(t)
                    copy_y(t, par, turn)

            def copy_hT(t):
                for a in range(2):
                    act.wait_ge(hT_in_psum, t * 2 + a + 1)
                    act.activation(hiddenT[:, 4 * a:4 * a + 4, :].rearrange("p k q -> p (k q)"), h_bank[a][:], ACT.Copy).then_inc(hT_ready, 1)

            def copy_y(t, par, turn):
                act.wait_ge(y_in_psum, t + 1)
                if not (isinstance(turn, int) and turn == 0):
                    act.wait_ge(y_stored[par], turn * 16)
                act.activation(y_rows[par][:], y_bank[:], ACT.Copy).then_inc(y_ready, 1)

            steps(act, tile)

        @block.vector
        def _(dve):
            def copy_xT(t, par):
                dve.wait_ge(xT_in_psum, t + 1)
                dve.tensor_copy(xT[par][:].rearrange("p k q -> p (k q)"), x_bank[:]).then_inc(xT_ready, 1)

            def tile(t, par, turn):
                for a in range(2):
                    dve.wait_ge(silu_ready, t * 2 + a + 1)
                    dve.tensor_tensor(hidden[par][:, a * 512:(a + 1) * 512], up_bank[:, a, :], gate[par][:, a * 512:(a + 1) * 512],
                                      ALU.mult).then_inc(hidden_ready, 1)
                if not (isinstance(t, int) and t == TILES - 1):
                    copy_xT(t + 1, 1 - par)
            copy_xT(0, 0)
            steps(dve, tile)

        @block.gpsimd
        def _(pool):
            def tile(t, par, turn):
                pool.wait_ge(y_ready, t + 1)
                pool.dma_start(S["y_rows"].rearrange("(t p) c -> t p c", p=P)[bass.ds(t, 1)].rearrange("a p c -> (a p) c"), y_rows[par][:]).then_inc(y_stored[par], 16)
            steps(pool, tile)
            for i in range(2):
                pool.wait_ge(y_stored[i], (TILES - i + 1) // 2 * 16)

        @block.tensor
        def _(pe):
            def turn_x(t, par, turn):
                pe.wait_ge(x_loaded[par], turn * 16 + 16)
                if not (isinstance(t, int) and t == 0):
                    pe.wait_ge(xT_ready, t)
                for k in range(KC):
                    mm = pe.transpose(x_bank[:, k * P:(k + 1) * P], x_rows[par][:, k * P:(k + 1) * P], T["ident"][:])
                mm.then_inc(xT_in_psum, 1)

            def gate_up(t, a, par, turn):
                if a == 0:
                    pe.wait_ge(xT_ready, t + 1)
                    pe.wait_ge(w_gu_loaded[par], turn * 16 + 16)
                if not (isinstance(t, int) and t == 0):
                    pe.wait_ge(hidden_ready, t * 2 - 1 + a)
                for bank, first in ((gate_bank, 0), (up_bank, F)):
                    for k in range(KC):
                        mm = pe.matmul(bank[:, a, :], xT[par][:, k, :], w_gu[par][:, k, first + a * 512:first + (a + 1) * 512],
                                       start=(k == 0), stop=(k == KC - 1))
                mm.then_inc(gu_in_psum, 1)

            def turn_hidden(t, par):
                for a in range(2):
                    pe.wait_ge(hidden_ready, t * 2 + a + 1)
                    for k in range(4):
                        f = 4 * a + k
                        mm = pe.transpose(h_bank[a][:, k * P:(k + 1) * P], hidden[par][:, f * P:(f + 1) * P], T["ident"][:])
                    mm.then_inc(hT_in_psum, 1)

            def down(t, par, turn):
                pe.wait_ge(w_down_loaded[par], turn * 16 + 16)
                if not (isinstance(t, int) and t == 0):
                    pe.wait_ge(y_ready, t)
                for f in range(FC):
                    if f % 4 == 0:
                        pe.wait_ge(hT_ready, t * 2 + f // 4 + 1)
                    mm = pe.matmul(y_bank[:], hiddenT[:, f, :], w_down[par][:, f, :], start=(f == 0), stop=(f == FC - 1))
                mm.then_inc(y_in_psum, 1)

            def tile(t, par, turn):
                first, last = isinstance(t, int) and t == 0, isinstance(t, int) and t == TILES - 1
                before = turn if par == 1 else turn - 1
                gate_up(t, 0, par, turn)
                if not first:
                    turn_hidden(t - 1, 1 - par)
                gate_up(t, 1, par, turn)
                if not last:
                    turn_x(t + 1, 1 - par, turn if par == 0 else turn + 1)
                if not first:
                    down(t - 1, 1 - par, before)
                if last:
                    turn_hidden(t, par)
                    down(t, par, turn)
            turn_x(0, 0, 0)
            steps(pe, tile)


def combine(nc, S, T):
    B, N, C, QH = S["B"], S["N"], S["C"], S["QH"]
    ROWS = 2 * B
    RING = 4
    with ExitStack() as ctx:
        def sb(n, shape, dt=F32):
            return ctx.enter_context(nc.sbuf_tensor(f"f_{n}", shape, dt))

        def sem(n):
            return ctx.enter_context(nc.semaphore(f"f_{n}"))
        y = [sb(f"y{i}", [QH, 2, C]) for i in range(RING)]
        std, rstd, eps = sb("std", [QH, ROWS]), sb("rstd", [QH, ROWS]), sb("eps", [QH, 1])
        gathered = [sem(f"gathered{i}") for i in range(RING)]
        added = sem("added")
        stats_ready = sem("stats_ready")
        var_ready = sem("var_ready")
        std_ready = sem("std_ready")
        rstd_ready = sem("rstd_ready")
        normed = sem("normed")
        stored = sem("stored")
        block = ctx.enter_context(nc.Block())

        @block.gpsimd
        def _(pool):
            for r in range(ROWS):
                if r >= RING:
                    pool.wait_ge(added, 2 * (r - RING) + 2)
                for i in range(2):
                    pool.indirect_dma_start(out=y[r % RING][:, i, :], out_offset=None, in_=S["y_rows"],
                                            in_offset=bass.IndirectOffsetOnAxis(ap=T["slot"][:, i, r:r + 1], axis=0)).then_inc(gathered[r % RING], 16)

        @block.vector
        def _(dve):
            dve.memset(eps[:], LN_EPS).then_inc(var_ready, 1)
            for r in range(ROWS):
                dve.wait_ge(gathered[r % RING], 32 * (r // RING + 1))
                for i in range(2):
                    dve.scalar_tensor_tensor(out=T["resid"][:, r, :], in0=y[r % RING][:, i, :], scalar=T["share"][:, i, r:r + 1],
                                             in1=T["resid"][:, r, :], op0=ALU.mult, op1=ALU.add).then_inc(added, 1)
                    dve.wait_ge(added, 2 * r + i + 1)
                dve.bn_stats(T["stats"][:, r, :], T["resid"][:, r, :]).then_inc(stats_ready, 1)
                dve.wait_ge(stats_ready, r + 1)
                dve.bn_aggr(T["mean_var"][:, r, :], T["stats"][:, r, :]).then_inc(var_ready, 1)
            dve.wait_ge(std_ready, 1)
            dve.reciprocal(rstd[:], std[:]).then_inc(rstd_ready, 1)
            dve.wait_ge(rstd_ready, 1)
            for r in range(ROWS):
                dve.tensor_scalar(T["resid"][:, r, :], T["resid"][:, r, :], T["mean_var"][:, r, 0:1], rstd[:, r:r + 1],
                                  ALU.subtract, ALU.mult).then_inc(normed, 1)

        @block.scalar
        def _(act):
            act.wait_ge(var_ready, ROWS + 1)
            act.activation(std[:], T["mean_var"][:, :, 1], ACT.Sqrt, bias=eps[:]).then_inc(std_ready, 1)

        @block.sync
        def _(sp):
            rows = S["out"].rearrange("b (h q) c -> (b h) q c", q=QH)
            for r in range(0, ROWS, 4):
                sp.wait_ge(normed, r + 4)
                sp.dma_start(rows[r:r + 4].rearrange("r q c -> q r c"), T["resid"][:, r:r + 4, :]).then_inc(stored, 16)
            sp.wait_ge(stored, ROWS // 4 * 16)


def build(nc, x, ctx_in, mask, Wqkv, Wproj, bproj, Wq, bq, Wk, bk, Wv, bv, Wo, bo, gate_w, gate_up_w, down_w, out):
    B, N, C = x.shape
    S = dict(x=x, ctx=ctx_in, mask=mask, Wqkv=Wqkv, Wproj=Wproj, bproj=bproj, Wq=Wq, bq=bq, Wk=Wk, bk=bk, Wv=Wv, bv=bv,
             Wo=Wo, bo=bo, gate_w=gate_w, gate_up_w=gate_up_w, down_w=down_w, out=out, B=B, N=N, C=C)
    S["H"] = 16
    S["HD"] = C // S["H"]
    S["W"] = 8
    S["QH"] = N // 2
    S["KW"] = S["QH"] + S["W"]
    S["KEY0"] = N - S["KW"]
    S["E"], S["F"] = down_w.shape[0:2]
    S["TILES"] = 2 * B * N // P + S["E"] - 1
    S["xT"] = nc.dram_tensor("xT_scratch", (2 * B, P, C // P, S["QH"]), F32, kind="Internal").ap()
    S["x_rows"] = nc.dram_tensor("x_rows_scratch", (S["TILES"] * P, C), F32, kind="Internal").ap()
    S["y_rows"] = nc.dram_tensor("y_rows_scratch", (S["TILES"] * P, C), F32, kind="Internal").ap()
    with ExitStack() as ctx:
        def sb(name, shape, dt=F32):
            return ctx.enter_context(nc.sbuf_tensor(name, shape, dt))
        QH, ROWS = S["QH"], 2 * B
        T = dict(ident=sb("ident", [P, P]), resid=sb("resid", [QH, ROWS, C]), stats=sb("stats", [QH, ROWS, 6]),
                 mean_var=sb("mean_var", [QH, ROWS, 2]), logits=sb("logits", [QH, ROWS, S["E"]]),
                 slot=sb("slot", [QH, 2, ROWS], U32), share=sb("top_share", [QH, 2, ROWS]), expert=sb("expert", [1, S["TILES"] + 1], I32),
                 changes=sb("changes", [1, S["TILES"] + 1], I32))
        with ExitStack() as actx:
            T["bias_row"] = actx.enter_context(nc.sbuf_tensor("bias_row", [QH, C], F32))
            T["zeros"] = actx.enter_context(nc.sbuf_tensor("zeros", [P, C], F32))
            T["band"] = actx.enter_context(nc.sbuf_tensor("band", [QH, 2, S["KW"]], F32))
            T["wqkv"] = actx.enter_context(nc.sbuf_tensor("wqkv", [P, C // P, 3 * C], F32))
            T["wproj"] = actx.enter_context(nc.sbuf_tensor("wproj", [P, C // P, C], F32))
            make_constants(nc, S, T)
            self_attention(nc, S, T)
        with ExitStack() as bctx:
            T["bias_row"] = bctx.enter_context(nc.sbuf_tensor("bias_row2", [QH, C], F32))
            normalise_and_turn(nc, S, T, "n1", bias=S["bo"])
        cross_attention(nc, S, T)
        normalise_and_turn(nc, S, T, "n2", router=True)
        route(nc, S, T)
        experts(nc, S, T)
        combine(nc, S, T)


_INS = ["x", "ctx_1024", "mask_BxSxS2_ik1", "L0_attn_Wqkv", "L0_attn_Wproj", "L0_attn_bproj", "L0_xattn_Wq", "L0_xattn_bq",
        "L0_xattn_Wk", "L0_xattn_bk", "L0_xattn_Wv", "L0_xattn_bv", "L0_xattn_Wo", "L0_xattn_bo", "L0_ffn_gate_w",
        "L0_ffn_gate_up_w", "L0_ffn_down_w"]


def kernel(**inputs):
    import numpy as _np
    import concourse.bacc as _bacc
    from concourse import mybir as _mybir
    from concourse.bass_utils import run_bass_kernel_spmd as _run

    nc = _bacc.Bacc("TRN2", target_bir_lowering=False, num_devices=1)
    arrays, args = {}, []
    for name in _INS:
        a = _np.ascontiguousarray(inputs[name])
        arrays[f"in_{name}_dram"] = a
        args.append(nc.dram_tensor(f"in_{name}_dram", a.shape, _mybir.dt.from_np(a.dtype), kind="ExternalInput").ap())
    args.append(nc.dram_tensor("out_dram", inputs["x"].shape, _mybir.dt.float32, kind="ExternalOutput").ap())
    build(nc, *args)
    r = _run(nc, [arrays], core_ids=[0])
    return r.results[0]["out_dram"]
```
